# Optimizing a Trainium2 kernel written in Bass

```python
import numpy as np
import jax
import jax.numpy as jnp

def _softmax(x, axis=-1):
    return jax.nn.softmax(x, axis=axis)

def _gelu(x):
    return jax.nn.gelu(x, approximate=True)

def _silu(x):
    return jax.nn.silu(x)

def _sigmoid(x):
    return jax.nn.sigmoid(x)

def _layernorm(x, axis=-1, eps=1e-05):
    m = jnp.mean(x, axis=axis, keepdims=True)
    v = jnp.var(x, axis=axis, keepdims=True)
    return (x - m) / jnp.sqrt(v + eps)

def _scatter_add(tgt, idx, src, axis=0):
    return tgt.at[idx].add(src)

def _segment_sum(src, seg, n):
    return jax.ops.segment_sum(src, seg, n)
kernel_name = 'mk_cond_seq_d2_seqx_r2_d5aec8'

def setup_inputs(seed: int=0):
    np.random.seed(seed)
    _w = jnp.asarray

    def _rec_inputs():
        import jax
        import jax.numpy as jnp
        _rk = jax.random.key(seed)
        x = 1.648e-05 + 1 * jax.random.normal(jax.random.fold_in(_rk, 1), (2, 2048, 512), jnp.float32)
        _lenS = 2048 - jax.random.randint(jax.random.fold_in(_rk, 7), (2,), 0, max(1, 2048 // 4) + 1, jnp.int32)
        _lenS2 = 2048 - jax.random.randint(jax.random.fold_in(_rk, 8), (2,), 0, max(1, 2048 // 4) + 1, jnp.int32)
        cond_1024 = 0.00191187 + 0.999416 * jax.random.normal(jax.random.fold_in(_rk, 11), (2, 512), jnp.float32)
        _validS = jnp.arange(2048)[None, :] < _lenS[:, None]
        _validS2 = jnp.arange(2048)[None, :] < _lenS2[:, None]
        _causal = jnp.tril(jnp.ones((2048, 2048), dtype=bool))
        mask_BxSxSx11_ik0 = jnp.where(jnp.ones((2, 2048, 2048, 11), dtype=bool), 0, 1).astype(jnp.int32)
        return (x, cond_1024, mask_BxSxSx11_ik0)
    x, cond_1024, mask_BxSxSx11_ik0 = _rec_inputs()

    def _L0_cond_setup():
        import jax, jax.numpy as jnp
        import numpy as np
        NONGT = 20
        H = 16
        NEG = -9000000000000000.0

        def _gat_attention(self_feat, cond_adj, label_bias, Wq, bq, Wk, bk, Wout, bout):
            B, N, F = self_feat.shape
            ng = min(NONGT, N)
            dh = F // H
            kv = self_feat[:, :ng]
            qh = (self_feat @ Wq.T + bq).reshape(B, N, H, dh)
            kh = (kv @ Wk.T + bk).reshape(B, ng, H, dh)
            aff = jnp.einsum('bnhd,bmhd->bnhm', qh, kh) * (1.0 / np.sqrt(dh))
            mask = cond_adj[:, :, None, :] > 0
            aff = jnp.where(mask, aff, NEG) + label_bias[:, :, None, :]
            w = jax.nn.softmax(aff, axis=-1)
            out_t = jnp.einsum('bnhm,bmf->bnhf', w, kv)
            out = jnp.einsum('bnhf,hgf->bnhg', out_t, Wout) + bout.reshape(H, F // H)
            return out.reshape(B, N, F)

        def _forward(v, q, adj, W_self, b_self, w_bias, b_bias, Wq, bq, Wk, bk, Wout, bout):
            adj_f = adj.astype(jnp.float32)
            exp_v = v
            row_zero = exp_v.sum(-1) == 0
            q_exp = jnp.where(row_zero[..., None], 0.0, q[:, None, :])
            vcq = jnp.concatenate([exp_v, q_exp], axis=-1)
            self_feat = vcq @ W_self.T + b_self
            output = self_feat
            for d in range(2):
                A = adj_f if d == 0 else jnp.swapaxes(adj_f, 1, 2)
                A = A[:, :, :NONGT, :]
                cond = A.sum(-1)
                vb = A @ w_bias + b_bias
                output = output + _gat_attention(self_feat, cond, vb, Wq[d], bq[d], Wk[d], bk[d], Wout[d], bout[d])
            rel = jax.nn.relu(output)
            return exp_v + rel
        key = jax.random.key(seed)
        ks = jax.random.split(key, 8)
        B, N, L, F, Q = (128, 36, 11, 512, 512)
        IN = F + Q
        s = 0.02
        return {'v': jax.random.normal(ks[0], (B, N, F), jnp.float32), 'q': jax.random.normal(ks[1], (B, Q), jnp.float32), 'adj': jax.random.randint(ks[2], (B, N, N, L), 0, 2, jnp.int32), 'W_self': jax.random.normal(ks[3], (F, IN), jnp.float32) * s, 'b_self': jnp.zeros((F,), jnp.float32), 'w_bias': jax.random.normal(ks[4], (L,), jnp.float32) * s, 'b_bias': jnp.zeros((), jnp.float32), 'Wq': jax.random.normal(ks[5], (2, F, F), jnp.float32) * s, 'bq': jnp.zeros((2, F), jnp.float32), 'Wk': jax.random.normal(ks[6], (2, F, F), jnp.float32) * s, 'bk': jnp.zeros((2, F), jnp.float32), 'Wout': jax.random.normal(ks[7], (2, H, F // H, F), jnp.float32) * s, 'bout': jnp.zeros((2, F), jnp.float32)}
    _L0_cond_all = _L0_cond_setup()
    _L0_cond_in = {k: v for k, v in _L0_cond_all.items() if k in ('W_self', 'b_self', 'w_bias', 'b_bias', 'Wq', 'bq', 'Wk', 'bk', 'Wout', 'bout')}
    del _L0_cond_all

    def _L1_cond_setup():
        import jax, jax.numpy as jnp
        import numpy as np
        D = 512
        H = 16
        HD = D // H
        MLP = 4 * D

        def _lin(key, fin, fout):
            k1, k2 = jax.random.split(key)
            lim = 1.0 / np.sqrt(fin)
            W = jax.random.uniform(k1, (fin, fout), minval=-lim, maxval=lim, dtype=jnp.float32)
            b = jax.random.uniform(k2, (fout,), minval=-lim, maxval=lim, dtype=jnp.float32)
            return (W, b)

        def layernorm(x, g, b, eps=1e-05):
            mu = jnp.mean(x, axis=-1, keepdims=True)
            var = jnp.var(x, axis=-1, keepdims=True)
            return (x - mu) * jax.lax.rsqrt(var + eps) * g + b

        def attention(h, Wqkv, bqkv, Wproj, bproj):
            B, L, _ = h.shape
            qkv = (h @ Wqkv + bqkv).reshape(B, L, 3, H, HD)
            q, k, v = jnp.moveaxis(qkv, 2, 0)
            scale = HD ** (-0.5)
            attn = jnp.einsum('blhd,bmhd->bhlm', q, k) * scale
            attn = jax.nn.softmax(attn, axis=-1)
            out = jnp.einsum('bhlm,bmhd->blhd', attn, v).reshape(B, L, D)
            return out @ Wproj + bproj
        key = jax.random.key(seed)
        ks = jax.random.split(key, 10)
        x = jax.random.normal(ks[0], (4, 1024, D), dtype=jnp.float32)
        time_emb = jax.random.normal(ks[1], (4, D), dtype=jnp.float32)
        Wqkv, bqkv = _lin(ks[2], D, 3 * D)
        Wproj, bproj = _lin(ks[3], D, D)
        W1, b1 = _lin(ks[4], D, MLP)
        W2, b2 = _lin(ks[5], MLP, D)
        Wt, bt = _lin(ks[6], D, 6 * D)
        g1 = jnp.ones((D,), jnp.float32)
        be1 = jnp.zeros((D,), jnp.float32)
        g2 = jnp.ones((D,), jnp.float32)
        be2 = jnp.zeros((D,), jnp.float32)
        return {'x': x, 'time_emb': time_emb, 'Wqkv': Wqkv, 'bqkv': bqkv, 'Wproj': Wproj, 'bproj': bproj, 'W1': W1, 'b1': b1, 'W2': W2, 'b2': b2, 'Wt': Wt, 'bt': bt, 'g1': g1, 'be1': be1, 'g2': g2, 'be2': be2}
    _L1_cond_all = _L1_cond_setup()
    _L1_cond_in = {k: v for k, v in _L1_cond_all.items() if k in ('Wqkv', 'bqkv', 'Wproj', 'bproj', 'W1', 'b1', 'W2', 'b2', 'Wt', 'bt', 'g1', 'be1', 'g2', 'be2')}
    del _L1_cond_all
    return {'x': x, 'cond_1024': cond_1024, 'mask_BxSxSx11_ik0': mask_BxSxSx11_ik0, 'L0_cond_W_self': _L0_cond_in['W_self'], 'L0_cond_b_self': _L0_cond_in['b_self'], 'L0_cond_w_bias': _L0_cond_in['w_bias'], 'L0_cond_b_bias': _L0_cond_in['b_bias'], 'L0_cond_Wq': _L0_cond_in['Wq'], 'L0_cond_bq': _L0_cond_in['bq'], 'L0_cond_Wk': _L0_cond_in['Wk'], 'L0_cond_bk': _L0_cond_in['bk'], 'L0_cond_Wout': _L0_cond_in['Wout'], 'L0_cond_bout': _L0_cond_in['bout'], 'L1_cond_Wqkv': _L1_cond_in['Wqkv'], 'L1_cond_bqkv': _L1_cond_in['bqkv'], 'L1_cond_Wproj': _L1_cond_in['Wproj'], 'L1_cond_bproj': _L1_cond_in['bproj'], 'L1_cond_W1': _L1_cond_in['W1'], 'L1_cond_b1': _L1_cond_in['b1'], 'L1_cond_W2': _L1_cond_in['W2'], 'L1_cond_b2': _L1_cond_in['b2'], 'L1_cond_Wt': _L1_cond_in['Wt'], 'L1_cond_bt': _L1_cond_in['bt'], 'L1_cond_g1': _L1_cond_in['g1'], 'L1_cond_be1': _L1_cond_in['be1'], 'L1_cond_g2': _L1_cond_in['g2'], 'L1_cond_be2': _L1_cond_in['be2']}

def reference(x, cond_1024, mask_BxSxSx11_ik0, L0_cond_W_self, L0_cond_b_self, L0_cond_w_bias, L0_cond_b_bias, L0_cond_Wq, L0_cond_bq, L0_cond_Wk, L0_cond_bk, L0_cond_Wout, L0_cond_bout, L1_cond_Wqkv, L1_cond_bqkv, L1_cond_Wproj, L1_cond_bproj, L1_cond_W1, L1_cond_b1, L1_cond_W2, L1_cond_b2, L1_cond_Wt, L1_cond_bt, L1_cond_g1, L1_cond_be1, L1_cond_g2, L1_cond_be2):
    import jax
    import jax.numpy as jnp

    def _L0_cond_ref(v, q, adj, W_self, b_self, w_bias, b_bias, Wq, bq, Wk, bk, Wout, bout):
        import jax, jax.numpy as jnp
        import numpy as np
        NONGT = 20
        H = 16
        NEG = -9000000000000000.0

        def _gat_attention(self_feat, cond_adj, label_bias, Wq, bq, Wk, bk, Wout, bout):
            B, N, F = self_feat.shape
            ng = min(NONGT, N)
            dh = F // H
            kv = self_feat[:, :ng]
            qh = (self_feat @ Wq.T + bq).reshape(B, N, H, dh)
            kh = (kv @ Wk.T + bk).reshape(B, ng, H, dh)
            aff = jnp.einsum('bnhd,bmhd->bnhm', qh, kh) * (1.0 / np.sqrt(dh))
            mask = cond_adj[:, :, None, :] > 0
            aff = jnp.where(mask, aff, NEG) + label_bias[:, :, None, :]
            w = jax.nn.softmax(aff, axis=-1)
            out_t = jnp.einsum('bnhm,bmf->bnhf', w, kv)
            out = jnp.einsum('bnhf,hgf->bnhg', out_t, Wout) + bout.reshape(H, F // H)
            return out.reshape(B, N, F)

        def _forward(v, q, adj, W_self, b_self, w_bias, b_bias, Wq, bq, Wk, bk, Wout, bout):
            adj_f = adj.astype(jnp.float32)
            exp_v = v
            row_zero = exp_v.sum(-1) == 0
            q_exp = jnp.where(row_zero[..., None], 0.0, q[:, None, :])
            vcq = jnp.concatenate([exp_v, q_exp], axis=-1)
            self_feat = vcq @ W_self.T + b_self
            output = self_feat
            for d in range(2):
                A = adj_f if d == 0 else jnp.swapaxes(adj_f, 1, 2)
                A = A[:, :, :NONGT, :]
                cond = A.sum(-1)
                vb = A @ w_bias + b_bias
                output = output + _gat_attention(self_feat, cond, vb, Wq[d], bq[d], Wk[d], bk[d], Wout[d], bout[d])
            rel = jax.nn.relu(output)
            return exp_v + rel
        return _forward(v, q, adj, W_self, b_self, w_bias, b_bias, Wq, bq, Wk, bk, Wout, bout)

    def _L1_cond_ref(x, time_emb, Wqkv, bqkv, Wproj, bproj, W1, b1, W2, b2, Wt, bt, g1, be1, g2, be2):
        import jax, jax.numpy as jnp
        import numpy as np
        D = 512
        H = 16
        HD = D // H
        MLP = 4 * D

        def _lin(key, fin, fout):
            k1, k2 = jax.random.split(key)
            lim = 1.0 / np.sqrt(fin)
            W = jax.random.uniform(k1, (fin, fout), minval=-lim, maxval=lim, dtype=jnp.float32)
            b = jax.random.uniform(k2, (fout,), minval=-lim, maxval=lim, dtype=jnp.float32)
            return (W, b)

        def layernorm(x, g, b, eps=1e-05):
            mu = jnp.mean(x, axis=-1, keepdims=True)
            var = jnp.var(x, axis=-1, keepdims=True)
            return (x - mu) * jax.lax.rsqrt(var + eps) * g + b

        def attention(h, Wqkv, bqkv, Wproj, bproj):
            B, L, _ = h.shape
            qkv = (h @ Wqkv + bqkv).reshape(B, L, 3, H, HD)
            q, k, v = jnp.moveaxis(qkv, 2, 0)
            scale = HD ** (-0.5)
            attn = jnp.einsum('blhd,bmhd->bhlm', q, k) * scale
            attn = jax.nn.softmax(attn, axis=-1)
            out = jnp.einsum('bhlm,bmhd->blhd', attn, v).reshape(B, L, D)
            return out @ Wproj + bproj
        tp = (jax.nn.silu(time_emb) @ Wt + bt)[:, None, :]
        shift_msa, scale_msa, gate_msa, shift_mlp, scale_mlp, gate_mlp = jnp.split(tp, 6, axis=-1)
        h = layernorm(x, g1, be1)
        h = h * (1.0 + scale_msa) + shift_msa
        h = attention(h, Wqkv, bqkv, Wproj, bproj)
        x = x + gate_msa * h
        h = layernorm(x, g2, be2)
        h = h * (1.0 + scale_mlp) + shift_mlp
        h = jax.nn.gelu(h @ W1 + b1, approximate=False) @ W2 + b2
        x = x + gate_mlp * h
        return x
    x = _L0_cond_ref(x, cond_1024, mask_BxSxSx11_ik0, L0_cond_W_self, L0_cond_b_self, L0_cond_w_bias, L0_cond_b_bias, L0_cond_Wq, L0_cond_bq, L0_cond_Wk, L0_cond_bk, L0_cond_Wout, L0_cond_bout)
    x = _L1_cond_ref(x, cond_1024, L1_cond_Wqkv, L1_cond_bqkv, L1_cond_Wproj, L1_cond_bproj, L1_cond_W1, L1_cond_b1, L1_cond_W2, L1_cond_b2, L1_cond_Wt, L1_cond_bt, L1_cond_g1, L1_cond_be1, L1_cond_g2, L1_cond_be2)
    return x

_drawn_inputs = setup_inputs


def setup_inputs(seed=0):
    import zlib

    import numpy as np

    out = dict(_drawn_inputs(seed))
    spreads = {'L0_cond_b_self': (0.0, 0.1),
     'L0_cond_bq': (0.0, 0.1),
     'L0_cond_bk': (0.0, 0.1),
     'L0_cond_bout': (0.0, 0.1),
     'L1_cond_g1': (1.0, 0.6),
     'L1_cond_be1': (0.0, 0.753),
     'L1_cond_g2': (1.0, 0.6),
     'L1_cond_be2': (0.0, 0.8)}
    factors = {'L1_cond_bqkv': 8.0,
     'L1_cond_bproj': 6.962,
     'L1_cond_b1': 8.0,
     'L1_cond_b2': 8.0,
     'L1_cond_bt': 7.324}
    for name, (base, spread) in spreads.items():
        noise = np.random.default_rng([zlib.crc32(name.encode()), seed]).standard_normal(out[name].shape)
        drawn = base * np.exp(spread * noise) if base else spread * noise
        out[name] = jnp.asarray(drawn.astype(out[name].dtype))
    for name, factor in factors.items():
        out[name] = (out[name] * factor).astype(out[name].dtype)
    return out
```

```python
import concourse.bass as bass
from concourse import mybir
from contextlib import ExitStack
import numpy as np

F32 = mybir.dt.float32
F32R = mybir.dt.float32r
I32 = mybir.dt.int32
ALU = mybir.AluOpType
ACT = mybir.ActivationFunctionType
AX = mybir.AxisListType

P = 128
B = 2
S = 2048
D = 512
DC = D // P
H = 16
HD = D // H
NONGT = 20
L = 11
HM = H * NONGT
HPC = P // HD
GM = HPC * NONGT
MLP = 4 * D
MC = MLP // P
NEG = -9000000000000000.0
SCALE = float(1.0 / np.sqrt(HD))
EPS = 1e-5
LO_HI = 2
PASSES = [(0, 0), (0, 1), (1, 0)]

COLS = {}
_at = 0
for _name, _n in [("cond", B * DC), ("b_self", DC), ("bq", 2 * DC), ("bk", 2 * DC), ("bqk", 2 * DC),
                  ("g", 2 * DC), ("be", 2 * DC), ("b1", MC), ("bt", 6 * DC)]:
    COLS[_name] = (_at, _n)
    _at += _n
NCOLS = _at
ROWS = ["b_self", "bout0", "bout1", "bt_gate_msa", "bt_gate_mlp", "bv", "bproj", "b2"]


def tiles(eng, n, unroll, body):
    for t in range(unroll):
        body(t, t)
    if n > 2 * unroll:
        with eng.Fori(1, n // unroll - 1) as i:
            for k in range(unroll):
                body(i * unroll + k, k)
    for t in range(max(n - unroll, unroll), n):
        body(t, t % unroll)


def at_least(t, n):
    return not isinstance(t, int) or t >= n


def before(t, n):
    return not isinstance(t, int) or t < n


def steps(eng, sem, first=0):
    count = [0]

    def link(ins):
        count[0] += 1
        ins.then_inc(sem, 1)
        eng.wait_ge(sem, first + count[0])
    return link


def raw(ap):
    return ap.bitcast(F32)


class Mem:

    def __init__(self, nc, ctx, tag):
        self.nc, self.ctx, self.tag, self.used = nc, ctx, tag, []

    def sb(self, name, shape, dt=F32):
        return self.ctx.enter_context(self.nc.sbuf_tensor(f"{self.tag}_{name}", shape, dt))

    def ps(self, name, shape=(P, 512), dt=F32):
        return self.ctx.enter_context(self.nc.psum_tensor(f"{self.tag}_{name}", list(shape), dt))

    def sem(self, name):
        self.used.append(self.nc.alloc_semaphore(f"{self.tag}_{name}"))
        return self.used[-1]

    def block(self):
        self.ctx.callback(self.retire)
        return self.ctx.enter_context(self.nc.Block())

    def retire(self):
        self.nc.clear_and_free_semaphores(self.used)
        self.nc.all_engine_barrier()

    def sems(self, name, n):
        return [self.sem(f"{name}{i}") for i in range(n)]


def setup_phase(nc, io, keep):
    with ExitStack() as ctx:
        m = Mem(nc, ctx, "set")
        NB = S // 512
        cols, ident = keep["cols"], keep["ident"]
        WsT = m.sb("WsT", [P, 2 * DC, D])
        Wsn = m.sb("Wsn", [P, DC, D])
        WkT_Gs = m.sb("WkT_Gs", [P, 2 * DC * B * HM])
        WkT = WkT_Gs[:, 0:2 * DC * D].rearrange("p (d c n) -> p d c n", d=2, c=DC)
        Gs = WkT_Gs[:].rearrange("p (d c b g) -> p d c b g", d=2, c=DC, b=B)
        Wq = m.sb("Wq", [P, 2, DC, D])
        WoT = Wq
        Wt = [m.sb(f"Wt{i}", [P, DC, D]) for i in range(2)]
        xT20 = m.sb("xT20", [P, DC, B, NONGT])
        e_cond = m.sb("e_cond", [P, DC * B])
        silu = m.sb("silu", [P, DC, B])
        silu_bc = m.sb("silu_bc", [P, B, DC, P])
        gate_b = m.sb("gate_b", [P, 2, D])
        gate0 = m.sb("gate0", [P, 2, D])
        tp = m.sb("tp", [P, 4 * DC, B])
        scale1 = m.sb("scale1", [P, 2, B, DC])
        moda, modb = m.sb("moda", [P, 2, B, DC]), m.sb("modb", [P, 2, B, DC])
        cq = m.sb("cq", [P, DC, B])
        qnz = m.sb("qnz", [P, DC, B, NONGT])
        sf20 = m.sb("sf20", [P, DC, B * NONGT])
        ones = m.sb("ones", [P, P])
        kt = m.sb("kt", [P, 2, DC, B * NONGT])
        Kblk = m.sb("Kblk", [P, 2, DC, B, GM])
        rows_in = m.sb("rows_in", [3, D])
        row = m.sb("row", [P, D + 2 * HM])
        row_parts = m.sb("row_parts", [P, 2, D + 2 * HM], F32R)
        vp = m.sb("vp", [P, D])
        pb = [m.ps(f"pb{i}") for i in range(8)]

        ld_small, ld_w, ld_k, ld_q, ld_o = [m.sem(x) for x in ("ld_small", "ld_w", "ld_k", "ld_q", "ld_o")]
        ld_t = m.sems("ld_t", 2)
        st = m.sem("st")
        e_ready, silu_ready, bc_ready, cleared = [m.sem(x) for x in ("e_ready", "silu_ready", "bc_ready", "cleared")]
        piece_done, gate_done, gate_ready = [m.sem(x) for x in ("piece_done", "gate_done", "gate_ready")]
        cq_done, cq_ready, sf_done, sf_ready = [m.sem(x) for x in ("cq_done", "cq_ready", "sf_done", "sf_ready")]
        kt_done, K_ready, G_done, G_ready = [m.sem(x) for x in ("kt_done", "K_ready", "G_done", "G_ready")]
        row_done, row_ready, parts_ready = [m.sem(x) for x in ("row_done", "row_ready", "parts_ready")]
        h_done, h_hi, h_lo, vp_done, vp_ready = [m.sem(x) for x in ("h_done", "h_hi", "h_lo", "vp_done", "vp_ready")]
        dv = m.sem("dv")
        w1_ready = m.sem("w1_ready")
        block = m.block()
        LW, VB, r4 = keep["LW"], keep["VB"], keep["r4"]

        def col(name, i=0, n=1):
            at = COLS[name][0] + i
            return cols[:, at:at + n]

        cond_v = col("cond", 0, B * DC).rearrange("p (c b) -> p c b", b=B)
        bt = COLS["bt"][0]
        tp_chunks = [0, 1, 2, 3, 4, 5, 6, 7, 12, 13, 14, 15, 16, 17, 18, 19]

        @block.sync
        def _(sp):
            sp.dma_start(cols[:], io["cols"]).then_inc(ld_small, 16)
            sp.dma_start(ident[:], io["ident"]).then_inc(ld_small, 16)
            sp.dma_start(keep["floor4"][:], io["floor4"]).then_inc(ld_small, 16)
            sp.dma_start(keep["wl_bc"][:], io["wl"][0:1, 0:2 * NONGT * L].to_broadcast([P, 2 * NONGT * L])).then_inc(ld_small, 16)
            sp.dma_start(keep["bb"][:], io["wl"][0:1, 2 * NONGT * L:2 * NONGT * L + 1].to_broadcast([P, 1])).then_inc(ld_small, 16)
            sp.dma_start(rows_in[:], io["rows"][0:3, :]).then_inc(ld_small, 16)
            for k in range(2):
                sp.dma_start(gate_b[:, k, :], io["rows"][3 + k:4 + k, :].to_broadcast([P, D])).then_inc(ld_small, 16)
            sp.dma_start(WsT[:], io["WselfT"].rearrange("(c p) n -> p c n", p=P)).then_inc(ld_w, 16)
            for b in range(B):
                sp.dma_start(xT20[:, :, b, :], io["xT"][b, :, 0:NONGT].rearrange("(c p) n -> p c n", p=P)).then_inc(ld_w, 16)
            wt_v = io["Wt"].rearrange("(c p) n -> p c n", p=P)
            for n in range(2):
                sp.dma_start(Wt[n][:], wt_v[:, :, n * D:(n + 1) * D]).then_inc(ld_t[n], 16)
            sp.dma_start(WkT, io["WkT"].rearrange("d (c p) n -> p d c n", p=P)).then_inc(ld_k, 16)
            sp.dma_start(Wq[:], io["Wq"].rearrange("d (c p) n -> p d c n", p=P)).then_inc(ld_q, 16)
            sp.dma_start(Wsn[:], io["Wself"][:, 0:D].rearrange("(c p) n -> p c n", p=P)).then_inc(ld_q, 16)
            for n in range(2, 6):
                sp.wait_ge(piece_done, n - 1)
                sp.dma_start(Wt[n % 2][:], wt_v[:, :, n * D:(n + 1) * D]).then_inc(ld_t[n % 2], 16)
            sp.wait_ge(G_done, 16)
            sp.dma_start(WoT[:], io["WoutT"].rearrange("d (c p) n -> p d c n", p=P)).then_inc(ld_o, 16)
            sp.wait_ge(gate_ready, 4)
            for k in range(2):
                for b in range(B):
                    for n in range(b * NB, (b + 1) * NB):
                        sp.dma_start(io["gate_d"][k, n], (gate_b if b else gate0)[:, k, :]).then_inc(st, 16)
            sp.wait_ge(parts_ready, 1)
            for b in range(B):
                for k in range(2):
                    for h in range(2):
                        at = 32 * (2 * k + b)
                        sp.dma_start(raw(r4[2 * k + h:2 * k + h + 1, b, :]), raw(row_parts[at:at + 1, h, :])).then_inc(st, 16)
            sp.wait_ge(cleared, 3)
            for b in range(B):
                for d in range(2):
                    sp.wait_ge(vp_ready, 2 * b + d + 1)
                    for r in range(HPC):
                        dst = VB[r * NONGT:(r + 1) * NONGT, b, d, :, r * HD:(r + 1) * HD]
                        at = 32 * (2 * b + d)
                        src = vp[at:at + NONGT, :].rearrange("p (j q) -> p j q", q=P)[:, :, r * HD:(r + 1) * HD]
                        sp.dma_start(dst, src).then_inc(st, 16)
            sp.wait_ge(st, 16 * (4 * NB + 8 + 16))

        @block.scalar
        def _(act):
            act.wait_ge(ld_small, 16 * 8)
            nc.scalar.activation(e_cond[:], col("cond", 0, B * DC), ACT.Exp, scale=-1.0).then_inc(e_ready, 1)
            n = 0
            for b in range(B):
                for d in range(2):
                    for ic in range(DC):
                        act.wait_ge(h_done, n + 1)
                        nc.scalar.activation(LW[:, 0, b, ic, D + d * HM:D + (d + 1) * HM], pb[n % 2][:, 0:HM],
                                             ACT.Identity).then_inc(h_hi, 1)
                        n += 1
            for n in range(4):
                act.wait_ge(vp_done, n + 1)
                nc.scalar.activation(vp[32 * n:32 * n + NONGT, :], pb[2 + n % 2][32 * n:32 * n + NONGT, :], ACT.Identity).then_inc(vp_ready, 1)

        @block.gpsimd
        def _(pool):
            nc.gpsimd.memset(VB[:], 0.0).then_inc(cleared, 1)
            nc.gpsimd.memset(Kblk[:], 0.0).then_inc(cleared, 1)
            nc.gpsimd.memset(ones[:], 1.0).then_inc(cleared, 1)
            pool.wait_ge(ld_w, 16 * 3)
            for b in range(B):
                nc.gpsimd.tensor_copy(LW[:, 0, b, :, 0:D], WsT[:, 0:DC, :]).then_inc(w1_ready, 1)
            for b in range(B):
                pool.wait_ge(w1_ready, B)
                nc.gpsimd.tensor_tensor(LW[:, 1, b, :, 0:D], WsT[:, 0:DC, :], LW[:, 0, b, :, 0:D], ALU.subtract).then_inc(w1_ready, 1)

        @block.vector
        def _(dve):
            link = steps(dve, dv)
            dve.wait_ge(ld_small, 16 * 8)
            dve.wait_ge(e_ready, 1)
            link(nc.vector.tensor_scalar_add(e_cond[:], e_cond[:], 1.0))
            link(nc.vector.reciprocal(e_cond[:], e_cond[:]))
            nc.vector.tensor_tensor(silu[:], cond_v, e_cond[:].rearrange("p (c b) -> p c b", b=B), ALU.mult).then_inc(silu_ready, 1)
            dve.wait_ge(silu_ready, 1)
            for b in range(B):
                nc.vector.tensor_copy(silu_bc[:, b], silu[:, :, b:b + 1].to_broadcast([P, DC, P])).then_inc(bc_ready, 1)
            dve.wait_ge(cq_done, 1)
            nc.vector.tensor_copy(cq[:], pb[0][:, 0:DC * B].rearrange("p (j b) -> p j b", b=B)).then_inc(cq_ready, 1)
            dve.wait_ge(cq_ready, 1)
            dve.wait_ge(sf_done, 1)
            for j in range(DC):
                for b in range(B):
                    last = nc.vector.tensor_scalar(qnz[:, j, b, :], pb[2][:, b * NONGT:(b + 1) * NONGT], 0.0,
                                                   cq[:, j, b:b + 1], ALU.not_equal, ALU.mult)
            link(last)
            for j in range(DC):
                last = nc.vector.scalar_tensor_tensor(sf20[:, j, :], pb[1][:, j * 40:(j + 1) * 40], col("b_self", j),
                                                      qnz[:, j].rearrange("p b m -> p (b m)"), ALU.add, ALU.add)
            last.then_inc(sf_ready, 1)
            dve.wait_ge(kt_done, 1)
            for d in range(2):
                for j in range(DC):
                    last = nc.vector.tensor_scalar(kt[:, d, j, :], pb[3][:, (d * DC + j) * 40:(d * DC + j + 1) * 40],
                                                   col("bk", d * DC + j), SCALE, ALU.add, ALU.mult)
            link(last)
            dve.wait_ge(cleared, 3)
            for r in range(HPC):
                dst = Kblk[r * HD:(r + 1) * HD, :, :, :, r * NONGT:(r + 1) * NONGT].rearrange("p d j b m -> p (d j) b m")
                src = kt[r * HD:(r + 1) * HD].rearrange("p d j (b m) -> p (d j) b m", m=NONGT)
                last = nc.vector.tensor_copy(dst, src)
            last.then_inc(K_ready, 1)
            for n in range(16):
                d, fc, half = n // 8, n // 2 % 4, n % 2
                dve.wait_ge(G_done, n + 1)
                dst = Gs[:, d, fc].rearrange("p b (j g) -> p j b g", g=GM)[:, 2 * half:2 * half + 2]
                src = pb[4 + n % 2][:, 0:4 * GM].rearrange("p (j b g) -> p j b g", j=2, b=B)
                nc.vector.tensor_copy(dst, src).then_inc(G_ready, 1)
            dve.wait_ge(piece_done, 2)
            dve.wait_ge(gate_done, 1)
            nc.vector.tensor_tensor(gate0[:, 0, :], pb[3][:], gate_b[:, 0, :], ALU.add).then_inc(gate_ready, 1)
            dve.wait_ge(piece_done, 3)
            nc.vector.tensor_tensor(gate_b[:, 0, :], pb[7][:], gate_b[:, 0, :], ALU.add).then_inc(gate_ready, 1)
            dve.wait_ge(piece_done, 5)
            for n, ch in enumerate(tp_chunks):
                last = nc.vector.tensor_scalar(tp[:, n, :], pb[6][:, n * B:(n + 1) * B], cols[:, bt + ch:bt + ch + 1], None, ALU.add)
            link(last)
            def per_chunk(ap):
                return ap.unsqueeze(2).to_broadcast([P, B, S // 512, DC])

            for k in range(2):
                g = col("g", k * DC, DC).unsqueeze(1).to_broadcast([P, B, DC])
                be = col("be", k * DC, DC).unsqueeze(1).to_broadcast([P, B, DC])
                shift = tp[:, 8 * k:8 * k + DC, :].rearrange("p c b -> p b c")
                scale = tp[:, 8 * k + DC:8 * k + 2 * DC, :].rearrange("p c b -> p b c")
                link(nc.vector.tensor_scalar_add(scale1[:, k], scale, 1.0))
                link(nc.vector.tensor_tensor(moda[:, k], scale1[:, k], g, ALU.mult))
                link(nc.vector.tensor_tensor(modb[:, k], scale1[:, k], be, ALU.mult))
                link(nc.vector.tensor_tensor(modb[:, k], modb[:, k], shift, ALU.add))
                for full, small in ((keep["modA"], moda), (keep["modB"], modb)):
                    nc.vector.tensor_copy(full[:, k].rearrange("p (b n c) -> p b n c", b=B, c=DC), per_chunk(small[:, k]))
            dve.wait_ge(gate_done, 2)
            nc.vector.tensor_tensor(gate0[:, 1, :], pb[3][:], gate_b[:, 1, :], ALU.add).then_inc(gate_ready, 1)
            dve.wait_ge(piece_done, 6)
            nc.vector.tensor_tensor(gate_b[:, 1, :], pb[7][:], gate_b[:, 1, :], ALU.add).then_inc(gate_ready, 1)
            for b in range(B):
                dve.wait_ge(row_done, 6 * b + 6)
                q, e = slice(32 * b, 32 * b + 1), slice(64 + 32 * b, 64 + 32 * b + 1)
                nc.vector.tensor_copy(row[q, 0:D], pb[0][q, :])
                nc.vector.tensor_copy(row[e, 0:D], pb[3][e, :])
                for d in range(2):
                    at = slice(D + d * HM, D + (d + 1) * HM)
                    nc.vector.tensor_copy(row[q, at], pb[1 + d][q, 0:HM])
                    last = nc.vector.tensor_copy(row[e, at], pb[4 + d][e, 0:HM])
                last.then_inc(row_ready, 1)
            dve.wait_ge(row_ready, 2)
            for k in range(4):
                at = slice(32 * k, 32 * k + 1)
                last = nc.vector.tensor_copy(row_parts[at, 0, :], row[at, :])
            link(last)
            for k in range(4):
                at = slice(32 * k, 32 * k + 1)
                last = nc.vector.tensor_tensor(row_parts[at, 1, :], row[at, :], row_parts[at, 0, :], ALU.subtract)
            last.then_inc(parts_ready, 1)
            n = 0
            for b in range(B):
                for d in range(2):
                    for ic in range(DC):
                        dve.wait_ge(h_hi, n + 1)
                        at = slice(D + d * HM, D + (d + 1) * HM)
                        nc.vector.tensor_tensor(LW[:, 1, b, ic, at], pb[n % 2][:, 0:HM], LW[:, 0, b, ic, at], ALU.subtract).then_inc(h_lo, 1)
                        n += 1

        @block.tensor
        def _(pe):
            def mm(out, a, b, first, last):
                return nc.tensor.matmul(out, a, b, start=first, stop=last)

            pe.wait_ge(ld_small, 16 * 8)
            pe.wait_ge(ld_w, 16 * 3)
            for j in range(DC):
                for c in range(DC):
                    last = mm(pb[0][:, j * B:(j + 1) * B], WsT[:, DC + c, j * P:(j + 1) * P], cond_v[:, c, :], c == 0, c == DC - 1)
            last.then_inc(cq_done, 1)
            for j in range(DC):
                for c in range(DC):
                    mm(pb[1][:, j * 40:(j + 1) * 40], WsT[:, c, j * P:(j + 1) * P],
                       xT20[:, c].rearrange("p b m -> p (b m)"), c == 0, c == DC - 1)
            pe.wait_ge(cleared, 3)
            for c in range(DC):
                last = mm(pb[2][:, 0:40], ones[:], xT20[:, c].rearrange("p b m -> p (b m)"), c == 0, c == DC - 1)
            last.then_inc(sf_done, 1)
            def modulation():
                pe.wait_ge(silu_ready, 1)
                pe.wait_ge(bc_ready, 2)
                for n in range(6):
                    pe.wait_ge(ld_t[n % 2], 16 * (n // 2 + 1))
                    if n % 3 < 2:
                        for j in range(DC):
                            at = (n - n // 3) * DC + j
                            for c in range(DC):
                                last = mm(pb[6][:, at * B:(at + 1) * B], Wt[n % 2][:, c, j * P:(j + 1) * P],
                                          silu[:, c, :], c == 0, c == DC - 1)
                        last.then_inc(piece_done, 1)
                    else:
                        if n == 5:
                            pe.wait_ge(gate_ready, 2)
                        for b in range(B):
                            for c in range(DC):
                                last = mm(pb[7 if b else 3][:], silu_bc[:, b, c, :], Wt[n % 2][:, c, :], c == 0, c == DC - 1)
                            if b == 0:
                                last.then_inc(gate_done, 1)
                        last.then_inc(piece_done, 1)

            pe.wait_ge(ld_k, 16)
            pe.wait_ge(sf_ready, 1)
            for d in range(2):
                for j in range(DC):
                    for c in range(DC):
                        last = mm(pb[3][:, (d * DC + j) * 40:(d * DC + j + 1) * 40], WkT[:, d, c, j * P:(j + 1) * P],
                                  sf20[:, c, :], c == 0, c == DC - 1)
            last.then_inc(kt_done, 1)
            pe.wait_ge(ld_q, 32)
            pe.wait_ge(K_ready, 1)
            for n in range(16):
                d, fc, half = n // 8, n // 2 % 4, n % 2
                if n >= 2:
                    pe.wait_ge(G_ready, n - 1)
                for k in range(2):
                    j = 2 * half + k
                    last = mm(pb[4 + n % 2][:, k * 2 * GM:(k + 1) * 2 * GM], Wq[:, d, j, fc * P:(fc + 1) * P],
                              Kblk[:, d, j].rearrange("p b g -> p (b g)"), True, True)
                last.then_inc(G_done, 1)
            modulation()
            pe.wait_ge(G_ready, 16)
            pe.wait_ge(cq_ready, 1)
            pe.wait_ge(gate_ready, 4)
            for b in range(B):
                q, e = slice(32 * b, 32 * b + 1), slice(64 + 32 * b, 64 + 32 * b + 1)
                if b:
                    pe.wait_ge(row_ready, b)
                for c in range(DC):
                    last = mm(pb[0][q, :], cond_v[:, c, b:b + 1], WsT[:, DC + c, :], c == 0, c == DC - 1)
                last.then_inc(row_done, 1)
                mm(pb[3][e, :], ones[0:3, 0:1], rows_in[:], True, True).then_inc(row_done, 1)
                for d in range(2):
                    for c in range(DC):
                        last = mm(pb[1 + d][q, 0:HM], cq[:, c, b:b + 1], Gs[:, d, c, b, :], c == 0, c == DC - 1)
                    last.then_inc(row_done, 1)
                    for c in range(DC):
                        mm(pb[4 + d][e, 0:HM], col("b_self", c), Gs[:, d, c, b, :], c == 0, c == DC - 1)
                    for j in range(DC):
                        last = nc.tensor.matmul(pb[4 + d][e, j * GM:(j + 1) * GM], col("bq", d * DC + j), Kblk[:, d, j, b, :],
                                                start=False, stop=True, skip_group_check=True)
                    last.then_inc(row_done, 1)
            pe.wait_ge(row_ready, 2)
            n = 0
            for b in range(B):
                for d in range(2):
                    for ic in range(DC):
                        if n >= 2:
                            pe.wait_ge(h_lo, n - 1)
                        for c in range(DC):
                            last = mm(pb[n % 2][:, 0:HM], Wsn[:, c, ic * P:(ic + 1) * P], Gs[:, d, c, b, :], c == 0, c == DC - 1)
                        last.then_inc(h_done, 1)
                        n += 1
            pe.wait_ge(ld_o, 16)
            for n in range(4):
                b, d = n // 2, n % 2
                if n >= 2:
                    pe.wait_ge(vp_ready, n - 1)
                for c in range(DC):
                    last = mm(pb[2 + n % 2][32 * n:32 * n + NONGT, :], sf20[:, c, b * NONGT:(b + 1) * NONGT], WoT[:, d, c, :], c == 0, c == DC - 1)
                last.then_inc(vp_done, 1)


def graph_phase(nc, io, keep):
    with ExitStack() as ctx:
        m = Mem(nc, ctx, "gat")
        NT = B * S // P
        NB = S // P
        LW, VB, r4, ident = keep["LW"], keep["VB"], keep["r4"], keep["ident"]
        MW = 2 * NONGT * L
        xT = [m.sb(f"xT{i}", [P, DC, P]) for i in range(2)]
        xs = [m.sb(f"xs{i}", [P, 2, DC, P], F32R) for i in range(2)]
        xrow = [m.sb(f"xrow{i}", [P, D]) for i in range(2)]
        msk = [m.sb(f"msk{i}", [P, MW], I32) for i in range(2)]
        mf = [m.sb(f"mf{i}", [P, MW]) for i in range(2)]
        mw = [m.sb(f"mw{i}", [P, MW]) for i in range(2)]
        onesr = m.sb("onesr", [P, P], F32R)
        zeros = m.sb("zeros", [P, 1, 1])
        n4 = [m.sb(f"n4{i}", [4, P], F32R) for i in range(2)]
        count = m.sb("count", [P, 2 * NONGT])
        vb = m.sb("vb", [P, 2 * NONGT])
        neg = m.sb("neg", [P, 2 * NONGT])
        open_ = m.sb("open", [P, 2 * NONGT])
        bias = m.sb("bias", [P, 2 * NONGT])
        aff = m.sb("aff", [P, 2, HM])
        prob = m.sb("prob", [P, 2, HM])
        top = m.sb("top", [P, 2 * H])
        total = m.sb("total", [P, 2 * H])
        wT = m.sb("wT", [GM, 2, DC * P])
        x1 = [m.sb(f"x1{i}", [P, D]) for i in range(2)]
        p_aff = m.ps("p_aff", [P, 2, 512])
        p_sf = [m.ps(f"p_sf{i}") for i in range(2)]
        p_wT = m.ps("p_wT", [P, 2, 512])
        p_n = m.ps("p_n")

        ones_ready = m.sem("ones_ready")
        loaded = m.sems("loaded", 2)
        row_loaded = m.sems("row_loaded", 2)
        stored = m.sems("stored", 2)
        x_split, x_part, mask_ready, mask_part = [m.sem(x) for x in ("x_split", "x_part", "mask_ready", "mask_part")]
        n_done, n_ready, aff_done, aff_read, sub_ready, exp_ready = [
            m.sem(x) for x in ("n_done", "n_ready", "aff_done", "aff_read", "sub_ready", "exp_ready")]
        w_ready, wT_done, wT_ready, att_done, x1_ready, mask_read, dv = [
            m.sem(x) for x in ("w_ready", "wT_done", "wT_ready", "att_done", "x1_ready", "mask_read", "dv")]
        block = m.block()
        xT_v = io["xT"].rearrange("b (c p) n -> p c b n", p=P)

        def per_batch(eng, body):
            for b in range(B):
                tiles(eng, NB, 2, lambda t, s: body(t + b * NB, s, b, t))

        @block.sync
        def _(sp):
            def load(t, s, b, tb):
                sp.dma_start(xT[s][:], xT_v[:, :, b, bass.ds(tb * P, P)]).then_inc(loaded[s], 16)
                sp.dma_start(msk[s][:], io["mask"][bass.ds(t * P, P), :]).then_inc(loaded[s], 16)

            def load_row(t, s):
                sp.dma_start(xrow[s][:], io["x"][bass.ds(t * P, P), :]).then_inc(row_loaded[s], 16)

            def store(t, s):
                sp.wait_ge(x1_ready, t + 1)
                sp.dma_start(io["x1_d"][bass.ds(t * P, P), :], x1[s][:]).then_inc(stored[s], 16)

            for t in range(2):
                load(t, t, 0, t)
                load_row(t, t)

            def body(t, s, b, tb):
                sp.wait_ge(x_split, t + 1)
                sp.wait_ge(mask_ready, t + 1)
                if before(tb, NB - 2):
                    load(t + 2, s, b, tb + 2)
                elif b + 1 < B:
                    load(t + 2, s, b + 1, tb + 2 - NB)
                if at_least(t, 1):
                    store(t - 1, 1 - s)
                    if before(t, NT - 1):
                        load_row(t + 1, 1 - s)
            per_batch(sp, body)
            store(NT - 1, 1)
            for s in range(2):
                sp.wait_ge(stored[s], 16 * NT // 2)

        @block.gpsimd
        def _(pool):
            nc.gpsimd.memset(zeros[:], 0.0).then_inc(ones_ready, 1)
            nc.gpsimd.memset(raw(onesr[:]), 1.0).then_inc(ones_ready, 1)
            pool.wait_ge(ones_ready, 2)

            def body(t, s, b, tb):
                pool.wait_ge(loaded[s], (t - s) * 16 + 32)
                if at_least(t, 2):
                    pool.wait_ge(aff_done, t - 1)
                if at_least(t, 2):
                    pool.wait_ge(mask_read, t - 1)
                nc.gpsimd.tensor_tensor(xs[s][:, 0], xT[s][:], zeros[:].to_broadcast([P, DC, P]), ALU.add).then_inc(x_part, 1)
                nc.gpsimd.tensor_copy(mf[s][:], msk[s][:]).then_inc(mask_part, 1)
                pool.wait_ge(x_part, t + 1)
                nc.gpsimd.tensor_tensor(xs[s][:, 1], xT[s][:], xs[s][:, 0], ALU.subtract).then_inc(x_split, 1)
                pool.wait_ge(mask_part, t + 1)
                nc.gpsimd.tensor_tensor(mw[s][:], mf[s][:], keep["wl_bc"][:], ALU.mult).then_inc(mask_ready, 1)
            per_batch(pool, body)

        @block.scalar
        def _(act):
            def body(t, s, b, tb):
                act.wait_ge(sub_ready, t + 1)
                nc.scalar.activation(prob[:], aff[:], ACT.Exp).then_inc(exp_ready, 1)
                act.wait_ge(wT_done, t + 1)
                if at_least(t, 1):
                    act.wait_ge(att_done, t)
                nc.scalar.activation(wT[:], p_wT[0:GM], ACT.Identity).then_inc(wT_ready, 1)
            per_batch(act, body)

        @block.vector
        def _(dve):
            NL = 6

            def mask_terms(t, s):
                link = steps(dve, dv, t * NL)
                dve.wait_ge(mask_ready, t + 1)
                nc.vector.tensor_reduce(count[:], mf[s][:].rearrange("p (k l) -> p k l", l=L), AX.X, ALU.add)
                nc.vector.tensor_reduce(vb[:], mw[s][:].rearrange("p (k l) -> p k l", l=L), AX.X, ALU.add).then_inc(mask_read, 1)
                dve.wait_ge(mask_read, t + 1)
                nc.vector.tensor_scalar(open_[:], count[:], 0.0, None, ALU.is_gt)
                link(nc.vector.tensor_scalar(neg[:], count[:], 0.0, NEG, ALU.is_le, ALU.mult))
                link(nc.vector.scalar_tensor_tensor(bias[:], vb[:], keep["bb"][:], neg[:], ALU.add, ALU.add))

            def row_flags(t, s):
                dve.wait_ge(n_done, t + 1)
                nc.vector.tensor_scalar(n4[s][:], p_n[0:4, 0:P], 0.0, keep["floor4"][:], ALU.not_equal, ALU.max).then_inc(n_ready, 1)

            def rest(t, s):
                dve.wait_ge(att_done, t + 1)
                dve.wait_ge(row_loaded[s], (t - s) * 8 + 16)
                if at_least(t, 2):
                    dve.wait_ge(stored[s], (t - s) * 8)
                nc.vector.scalar_tensor_tensor(x1[s][:], p_sf[s][:], 0.0, xrow[s][:], ALU.max, ALU.add).then_inc(x1_ready, 1)

            mask_terms(0, 0)
            row_flags(0, 0)

            def body(t, s, b, tb):
                link = steps(dve, dv, t * NL + 2)

                def heads(ap):
                    return ap.rearrange("p (d m) -> p d m", d=2).unsqueeze(2).to_broadcast([P, 2, H, NONGT])

                def of_head(ap):
                    return ap.rearrange("p (d h) -> p d h", d=2).unsqueeze(3).to_broadcast([P, 2, H, NONGT])

                a4 = aff[:].rearrange("p d (h m) -> p d h m", m=NONGT)
                dve.wait_ge(aff_done, t + 1)
                if at_least(t, 1):
                    dve.wait_ge(exp_ready, t)
                nc.vector.tensor_tensor(a4, p_aff[:, :, 0:HM].rearrange("p d (h m) -> p d h m", m=NONGT),
                                        heads(open_[:]), ALU.mult).then_inc(aff_read, 1)
                dve.wait_ge(aff_read, t + 1)
                link(nc.vector.tensor_tensor(a4, a4, heads(bias[:]), ALU.add))
                link(nc.vector.tensor_reduce(top[:], aff[:].rearrange("p d (h m) -> p (d h) m", m=NONGT), AX.X, ALU.max))
                nc.vector.tensor_tensor(a4, a4, of_head(top[:]), ALU.subtract).then_inc(sub_ready, 1)
                if before(t, NT - 1):
                    row_flags(t + 1, 1 - s)
                if at_least(t, 1):
                    rest(t - 1, 1 - s)
                p4 = prob[:].rearrange("p d (h m) -> p d h m", m=NONGT)
                dve.wait_ge(exp_ready, t + 1)
                link(nc.vector.tensor_reduce(total[:], prob[:].rearrange("p d (h m) -> p (d h) m", m=NONGT), AX.X, ALU.add))
                link(nc.vector.reciprocal(total[:], total[:]))
                nc.vector.tensor_tensor(p4, p4, of_head(total[:]), ALU.mult).then_inc(w_ready, 1)
                if before(t, NT - 1):
                    mask_terms(t + 1, 1 - s)
            per_batch(dve, body)
            rest(NT - 1, 1)

        @block.tensor
        def _(pe):
            pe.wait_ge(ones_ready, 2)

            def products(t, s, b):
                pe.wait_ge(x_split, t + 1)
                if at_least(t, 1):
                    pe.wait_ge(n_ready, t)
                for k in range(2):
                    for c in range(DC):
                        last = nc.tensor.matmul(p_n[:, 0:P], onesr[:], xs[s][:, k, c, :], start=k + c == 0, stop=k + c == DC)
                last.then_inc(n_done, 1)
                if at_least(t, 2):
                    pe.wait_ge(x1_ready, t - 1)
                if at_least(t, 1):
                    pe.wait_ge(aff_read, t)
                outs = [(p_sf[s][:], slice(0, D)), (p_aff[:, 0, 0:HM], slice(D, D + HM)), (p_aff[:, 1, 0:HM], slice(D + HM, D + 2 * HM))]
                for k, w in PASSES:
                    for c in range(DC):
                        for o, at in outs:
                            nc.tensor.matmul(o, xs[s][:, k, c, :], LW[:, w, b, c, at], start=(k + w + c == 0), stop=False)
                pe.wait_ge(n_ready, t + 1)
                for n, (o, at) in enumerate(outs):
                    last = nc.tensor.matmul(o, n4[s][:], r4[:, b, at], start=False, stop=True)
                last.then_inc(aff_done, 1)

            products(0, 0, 0)

            def body(t, s, b, tb):
                if before(tb, NB - 1):
                    products(t + 1, 1 - s, b)
                elif b + 1 < B:
                    products(t + 1, 1 - s, b + 1)
                pe.wait_ge(w_ready, t + 1)
                if at_least(t, 1):
                    pe.wait_ge(wT_ready, t)
                for d in range(2):
                    for j in range(DC):
                        last = nc.tensor.transpose(p_wT[0:GM, d, j * P:(j + 1) * P], prob[:, d, j * GM:(j + 1) * GM], ident[:])
                last.then_inc(wT_done, 1)
                pe.wait_ge(wT_ready, t + 1)
                for d in range(2):
                    for j in range(DC):
                        last = nc.tensor.matmul(p_sf[s][:, j * P:(j + 1) * P], wT[:, d, j * P:(j + 1) * P], VB[:, b, d, j, :],
                                                start=False, stop=True, skip_group_check=True)
                last.then_inc(att_done, 1)
            per_batch(pe, body)


def norm_rows(nc, dve, link, x, stats, mv, rstd, tmp, var_ready, root_ready, n):
    ve, r = tmp[:, 0:4], rstd[:]
    for nt in range(3):
        last = nc.vector.bn_stats(stats[:, nt, :], x[:, nt, :])
    link(last)
    nc.vector.bn_stats(stats[:, 3, :], x[:, 3, :])
    for nt in range(3):
        last = nc.vector.bn_aggr(mv[:, nt, :], stats[:, nt, :])
    link(last)
    nc.vector.tensor_scalar_add(ve[:, 0:3], mv[:, 0:3, 1], EPS)
    link(nc.vector.bn_aggr(mv[:, 3, :], stats[:, 3, :]))
    nc.vector.tensor_scalar_add(ve[:, 3:4], mv[:, 3:4, 1], EPS).then_inc(var_ready, 1)
    dve.wait_ge(root_ready, n + 1)
    link(nc.vector.reciprocal(r, tmp[:, 4:8]))
    link(nc.vector.tensor_tensor(tmp[:, 8:12], r, r, ALU.mult))
    link(nc.vector.tensor_tensor(tmp[:, 8:12], tmp[:, 8:12], ve, ALU.mult))
    link(nc.vector.tensor_scalar(tmp[:, 8:12], tmp[:, 8:12], -0.5, 1.5, ALU.mult, ALU.add))
    link(nc.vector.tensor_tensor(r, r, tmp[:, 8:12], ALU.mult))


NORM_LINKS = 8


def qkv_phase(nc, io, keep):
    with ExitStack() as ctx:
        m = Mem(nc, ctx, "qkv")
        NCH = B * S // 512
        cols, ident, modA, modB = keep["cols"], keep["ident"], keep["modA"], keep["modB"]
        stage = m.sb("stage", [P, DC, 3 * D])
        W = m.sb("W", [P, 2, DC, 3 * D], F32R)
        bv = m.sb("bv", [P, D])
        xr = [m.sb(f"xr{i}", [P, 4, D]) for i in range(2)]
        xn = m.sb("xn", [P, 4, D])
        th = [m.sb(f"th{i}", [P, 512]) for i in range(2)]
        hs = [m.sb(f"hs{i}", [P, 2, DC, 512], F32R) for i in range(2)]
        tq = [m.sb(f"tq{i}", [P, 512]) for i in range(2)]
        qs = [m.sb(f"qs{i}", [P, 2, 512], F32R) for i in range(4)]
        vs = [m.sb(f"vs{i}", [P, 512]) for i in range(2)]
        stats, mv = m.sb("stats", [P, 4, 6]), m.sb("mv", [P, 4, 2])
        rstd, tmp = m.sb("rstd", [P, 4]), m.sb("tmp", [P, 12])
        pT = [m.ps(f"pT{i}") for i in range(2)]
        pq = [m.ps(f"pq{i}") for i in range(4)]
        pv = [m.ps(f"pv{i}") for i in range(2)]

        w_loaded = m.sems("w_loaded", DC)
        b_loaded, w_hi, w_lo = [m.sem(x) for x in ("b_loaded", "w_hi", "w_lo")]
        x_loaded, q_stored, v_stored = m.sems("x_loaded", 2), m.sems("q_stored", 4), m.sems("v_stored", 2)
        var_ready, root_ready, xn_ready, tr_done, h_hi, h_lo = [
            m.sem(x) for x in ("var_ready", "root_ready", "xn_ready", "tr_done", "h_hi", "h_lo")]
        q_done, q_hi, q_lo, v_done, v_ready, dv, ac = [
            m.sem(x) for x in ("q_done", "q_hi", "q_lo", "v_done", "v_ready", "dv", "ac")]
        block = m.block()
        ORDER = [("q", 0), ("q", 1), ("h", 0), ("q", 2), ("h", 1), ("q", 3), ("h", 2), ("q", 4), ("h", 3),
                 ("q", 5), ("q", 6), ("q", 7), ("v", 0), ("v", 1), ("v", 2), ("v", 3)]
        x_v = io["x1_d"].rearrange("(n p) d -> p n d", p=P)

        @block.sync
        def _(sp):
            def load(i, s):
                sp.dma_start(xr[s][:], x_v[:, bass.ds(i * 4, 4), :]).then_inc(x_loaded[s], 16)

            load(0, 0)
            for c in range(DC):
                sp.dma_start(stage[:, c, :], io["Wqkv"][c * P:(c + 1) * P, :]).then_inc(w_loaded[c], 16)
            sp.dma_start(bv[:], io["rows"][5:6, :].to_broadcast([P, D])).then_inc(b_loaded, 16)
            load(1, 1)

            def body(i, s):
                if before(i, NCH - 2):
                    sp.wait_ge(xn_ready, i + 1)
                    load(i + 2, s)
                for kind, j in ORDER:
                    if kind == "q":
                        sp.wait_ge(q_lo, i * 8 + j + 1)
                        dst = io["qk_d"][j // 4, :, (j % 4) * P:(j % 4 + 1) * P, bass.ds(i * 512, 512)]
                        sp.dma_start(dst.rearrange("a p n -> p a n"), raw(qs[j % 4][:])).then_inc(q_stored[j % 4], 16)
                    elif kind == "v":
                        sp.wait_ge(v_ready, i * 4 + j + 1)
                        sp.dma_start(io["v_d"][bass.ds(i * 512 + j * P, P), :], vs[j % 2][:]).then_inc(v_stored[j % 2], 16)
            tiles(sp, NCH, 2, body)
            for x in q_stored:
                sp.wait_ge(x, 16 * 2 * NCH)
            for x in v_stored:
                sp.wait_ge(x, 16 * 2 * NCH)

        @block.scalar
        def _(act):
            for c in range(DC):
                act.wait_ge(w_loaded[c], 16)
                nc.scalar.activation(W[:, 0, c, :], stage[:, c, :], ACT.Identity).then_inc(w_hi, 1)

            def root(i):
                act.wait_ge(var_ready, i + 1)
                nc.scalar.activation(tmp[:, 4:8], tmp[:, 0:4], ACT.Sqrt).then_inc(root_ready, 1)

            def h_parts(i, s, c):
                act.wait_ge(tr_done, i * 4 + c + 1)
                if c >= 2 or at_least(i, 1):
                    act.wait_ge(h_lo, i * 4 + c - 1)
                if c == 0 and at_least(i, 2):
                    act.wait_ge(v_done, i * 4 - 4)
                a, b = modA[:, 0, bass.ds(i * DC + c, 1)], modB[:, 0, bass.ds(i * DC + c, 1)]
                nc.scalar.activation(th[c % 2][:], pT[c % 2][:], ACT.Identity, bias=b, scale=a)
                nc.scalar.activation(hs[s][:, 0, c, :], pT[c % 2][:], ACT.Identity, bias=b, scale=a).then_inc(h_hi, 1)

            root(0)
            for c in range(DC):
                h_parts(0, 0, c)

            def body(i, s):
                if before(i, NCH - 1):
                    root(i + 1)
                for kind, j in ORDER:
                    if kind == "q":
                        n = i * 8 + j
                        act.wait_ge(q_done, n + 1)
                        if j >= 2 or at_least(i, 1):
                            act.wait_ge(q_lo, n - 1)
                        if j >= 4 or at_least(i, 1):
                            act.wait_ge(q_stored[j % 4], (i * 2 + j // 4) * 16)
                        bias = cols[:, COLS["bqk"][0] + j:COLS["bqk"][0] + j + 1]
                        nc.scalar.activation(tq[j % 2][:], pq[j % 4][:], ACT.Identity, bias=bias)
                        nc.scalar.activation(qs[j % 4][:, 0, :], pq[j % 4][:], ACT.Identity, bias=bias).then_inc(q_hi, 1)
                    elif kind == "h" and before(i, NCH - 1):
                        h_parts(i + 1, 1 - s, j)
            tiles(act, NCH, 2, body)

        @block.vector
        def _(dve):
            def norm(i, s):
                link = steps(dve, dv, i * NORM_LINKS)
                dve.wait_ge(x_loaded[s], (i - s) * 8 + 16)
                norm_rows(nc, dve, link, xr[s], stats, mv, rstd, tmp, var_ready, root_ready, i)
                if at_least(i, 1):
                    dve.wait_ge(tr_done, i * 4)
                for nt in range(4):
                    last = nc.vector.tensor_scalar(xn[:, nt, :], xr[s][:, nt, :], mv[:, nt, 0:1], rstd[:, nt:nt + 1],
                                                   ALU.subtract, ALU.mult)
                last.then_inc(xn_ready, 1)

            def h_low(i, s, c):
                dve.wait_ge(h_hi, i * 4 + c + 1)
                nc.vector.tensor_tensor(hs[s][:, 1, c, :], th[c % 2][:], hs[s][:, 0, c, :], ALU.subtract).then_inc(h_lo, 1)

            norm(0, 0)
            for c in range(DC):
                dve.wait_ge(w_hi, c + 1)
                nc.vector.tensor_tensor(W[:, 1, c, :], stage[:, c, :], W[:, 0, c, :], ALU.subtract).then_inc(w_lo, 1)
            for c in range(DC):
                h_low(0, 0, c)
            dve.wait_ge(b_loaded, 16)

            def body(i, s):
                if before(i, NCH - 1):
                    norm(i + 1, 1 - s)
                for kind, j in ORDER:
                    if kind == "q":
                        dve.wait_ge(q_hi, i * 8 + j + 1)
                        nc.vector.tensor_tensor(qs[j % 4][:, 1, :], tq[j % 2][:], qs[j % 4][:, 0, :], ALU.subtract).then_inc(q_lo, 1)
                    elif kind == "h":
                        if before(i, NCH - 1):
                            h_low(i + 1, 1 - s, j)
                    else:
                        dve.wait_ge(v_done, i * 4 + j + 1)
                        if j >= 2 or at_least(i, 1):
                            dve.wait_ge(v_stored[j % 2], (i * 2 + j // 2) * 16)
                        nc.vector.tensor_tensor(vs[j % 2][:], pv[j % 2][:], bv[:], ALU.add).then_inc(v_ready, 1)
            tiles(dve, NCH, 2, body)

        @block.tensor
        def _(pe):
            def transposes(i, c):
                if c == 0:
                    pe.wait_ge(xn_ready, i + 1)
                if c >= 2 or at_least(i, 1):
                    pe.wait_ge(h_hi, i * 4 + c - 1)
                for nt in range(4):
                    last = nc.tensor.transpose(pT[c % 2][:, nt * P:(nt + 1) * P], xn[:, nt, c * P:(c + 1) * P], ident[:])
                last.then_inc(tr_done, 1)

            for c in range(DC):
                transposes(0, c)
            pe.wait_ge(w_lo, DC)

            def body(i, s):
                pe.wait_ge(h_lo, i * 4 + 4)
                for kind, j in ORDER:
                    if kind == "h":
                        if before(i, NCH - 1):
                            transposes(i + 1, j)
                        continue
                    if kind == "q":
                        if j >= 4 or at_least(i, 1):
                            pe.wait_ge(q_hi, i * 8 + j - 3)
                        out, done = pq[j % 4], q_done
                    else:
                        if j >= 2 or at_least(i, 1):
                            pe.wait_ge(v_ready, i * 4 + j - 1)
                        out, done = pv[j % 2], v_done
                    for n, (k, w) in enumerate(PASSES):
                        for c in range(DC):
                            if kind == "q":
                                a, r = W[:, k, c, j * P:(j + 1) * P], hs[s][:, w, c, :]
                            else:
                                a, r = hs[s][:, k, c, j * P:(j + 1) * P], W[:, w, c, 2 * D:3 * D]
                            last = nc.tensor.matmul(out[:], a, r, start=n + c == 0, stop=n == 2 and c == DC - 1)
                    last.then_inc(done, 1)
            tiles(pe, NCH, 2, body)


def attention_phase(nc, io, keep):
    with ExitStack() as ctx:
        m = Mem(nc, ctx, "att")
        NG = B * H // 2
        ST = 32
        KD = 3 * HD
        NM = 2 * 16 * 4
        MBY = 30
        U = 4
        ident = keep["ident"]
        qs = [m.sb(f"qs{i}", [KD + 2, 2, S], F32R) for i in range(U)]
        ks = [m.sb(f"ks{i}", [KD + 2, 2, S], F32R) for i in range(U)]
        V = [m.sb(f"V{i}", [P, 16, 2 * HD]) for i in range(2)]
        ones = m.sb("ones", [P, HD])
        prob = [m.sb(f"prob{i}", [P, 4, 512]) for i in range(4)]
        mx = m.sb("mx", [P, 32, 4])
        top = m.sb("top", [P, 32])
        nm = m.sb("nm", [32, 2, P], F32R)
        rec, o = m.sb("rec", [P, 512]), m.sb("o", [P, 512])
        os_ = [m.sb(f"os{i}", [P, 2, 512], F32R) for i in range(2)]
        zero = m.sb("zero", [P, 1])
        pS = [m.ps(f"pS{i}") for i in range(3)]
        pM = [m.ps(f"pM{i}") for i in range(3)]
        pO, pZ = m.ps("pO"), m.ps("pZ")

        loaded, v_loaded, o_stored = m.sems("loaded", U), m.sems("v_loaded", 2), m.sems("o_stored", 2)
        cleared, s_done, exp_done, m_done, m_read = [m.sem(x) for x in ("cleared", "s_done", "exp_done", "m_done", "m_read")]
        top_ready, pv_done, o_read, o_hi, o_lo, dv, dv2 = [
            m.sem(x) for x in ("top_ready", "pv_done", "o_read", "o_hi", "o_lo", "nm_hi", "rec_ready")]
        top_rows = m.sems("top_rows", U)
        block = m.block()
        q_v = io["qk_d"][0].rearrange("a (g h p) n -> a g p h n", h=2, p=HD)
        k_v = io["qk_d"][1].rearrange("a (g h p) n -> a g p h n", h=2, p=HD)
        v_v = io["v_d"].rearrange("(b t p) d -> p b t d", b=B, p=P)
        o_v = io["o_d"].rearrange("a (g h p) (b n) -> g h p a b n", h=2, p=HD, b=B)

        def m_units(step):
            return range(min(NM, step * NM // MBY), min(NM, (step + 1) * NM // MBY))

        def groups(eng, body):
            for g in range(U):
                body(g, g, g // 2)
            with eng.Fori(1, NG // U - 1) as i:
                for k in range(U):
                    body(i * U + k, k, i * (U // 2) + k // 2)
            for g in range(NG - U, NG):
                body(g, g % U, g // 2)

        @block.sync
        def _(sp):
            def load(g, k, hp):
                b = k % 2
                at = slice(b * S, (b + 1) * S)
                for i, part in enumerate((0, 0, 1)):
                    sp.dma_start(raw(qs[k][i * HD:(i + 1) * HD]), q_v[part, bass.ds(hp, 1), :, :, at]
                                 .rearrange("a p h n -> (a p) h n")).then_inc(loaded[k], 16)
                for i, part in enumerate((0, 1, 0)):
                    sp.dma_start(raw(ks[k][i * HD:(i + 1) * HD]), k_v[part, bass.ds(hp, 1), :, :, at]
                                 .rearrange("a p h n -> (a p) h n")).then_inc(loaded[k], 16)

            def load_v(g, k, hp):
                sp.dma_start(V[k % 2][:], v_v[:, k % 2, :, bass.ds(hp * 2 * HD, 2 * HD)]).then_inc(v_loaded[k % 2], 16)

            def rows(g, k):
                sp.wait_ge(m_read, (g + 1) * (NM + 1))
                for h in range(2):
                    sp.dma_start(raw(qs[k][KD + h:KD + h + 1]).rearrange("a h (t n) -> a (h t) n", n=P),
                                 raw(nm[:, h, :])).then_inc(top_rows[k], 16)

            load(0, 0, 0)
            load_v(0, 0, 0)
            load(1, 1, 0)
            load_v(1, 1, 0)
            load(2, 2, 1)
            load(3, 3, 1)
            rows(0, 0)

            def store(g, k, hp, lp):
                sp.wait_ge(o_lo, g * 2 + lp + 1)
                for c in range(4):
                    dst = o_v[bass.ds(hp, 1), c // 2, :, :, k % 2, (2 * lp + c % 2) * 512:(2 * lp + c % 2 + 1) * 512]
                    sp.dma_start(dst.rearrange("g p a n -> (g p) a n"), raw(os_[lp][c * HD:(c + 1) * HD])).then_inc(o_stored[lp], 16)

            def body(g, k, hp):
                store(g, k, hp, 0)
                if before(g, NG - 1):
                    rows(g + 1, (k + 1) % U)
                store(g, k, hp, 1)
                sp.wait_ge(pv_done, g * ST + ST)
                if before(g, NG - U):
                    load(g + U, k, hp + U // 2)
                if before(g, NG - 2):
                    load_v(g + 2, k + 2, hp + 1)
            groups(sp, body)
            for x in o_stored:
                sp.wait_ge(x, 16 * 4 * NG)

        @block.gpsimd
        def _(pool):
            nc.gpsimd.memset(ones[:], 1.0).then_inc(cleared, 1)
            nc.gpsimd.memset(zero[:], 0.0).then_inc(cleared, 1)
            for k in range(U):
                pool.wait_ge(cleared, 2 + k)
                nc.gpsimd.memset(raw(ks[k][KD:KD + 2]), 1.0).then_inc(cleared, 1)
            pool.wait_ge(cleared, 2 + U)

            def body(g, k, hp):
                for lp in range(2):
                    pool.wait_ge(o_read, g * 2 + lp + 1)
                    if at_least(g, 1):
                        pool.wait_ge(o_stored[lp], g * 64)
                    nc.gpsimd.tensor_tensor(os_[lp][:, 0, :], o[:], zero[:].to_broadcast([P, 512]), ALU.add).then_inc(o_hi, 1)
                    pool.wait_ge(o_hi, g * 2 + lp + 1)
                    nc.gpsimd.tensor_tensor(os_[lp][:, 1, :], o[:], os_[lp][:, 0, :], ALU.subtract).then_inc(o_lo, 1)
            groups(pool, body)

        @block.scalar
        def _(act):
            def body(g, k, hp):
                for step in range(ST):
                    if step >= 4 or at_least(g, 1):
                        act.wait_ge(pv_done, g * ST + step - 3)
                    for c in range(4):
                        n = 4 * step + c
                        act.wait_ge(s_done, g * 4 * ST + n + 1)
                        nc.scalar.activation(prob[step % 4][:, c, :], pS[n % 3][:], ACT.Exp, scale=SCALE).then_inc(exp_done, 1)
            groups(act, body)

        @block.vector
        def _(dve):
            def maxima(g, units):
                for n in units:
                    dve.wait_ge(m_done, g * (NM + 1) + n + 1)
                    nc.vector.tensor_reduce(mx[:, n // 4, n % 4:n % 4 + 1], pM[n % 3][:], AX.X, ALU.max).then_inc(m_read, 1)

            def top_of(g):
                dve.wait_ge(m_read, g * (NM + 1) + NM)
                nc.vector.tensor_reduce(top[:], mx[:], AX.X, ALU.max, negate=True).then_inc(top_ready, 1)

            def parts(g, k):
                dve.wait_ge(m_done, g * (NM + 1) + NM + 1)
                if at_least(g, 1):
                    dve.wait_ge(top_rows[(k - 1) % U], (g - 1 - (k - 1) % U) * 8 + 32)
                nc.vector.tensor_copy(nm[:, 0, :], pM[NM % 3][0:32, 0:P]).then_inc(dv, 1)
                dve.wait_ge(dv, g + 1)
                nc.vector.tensor_tensor(nm[:, 1, :], pM[NM % 3][0:32, 0:P], nm[:, 0, :], ALU.subtract).then_inc(m_read, 1)

            maxima(0, range(NM))
            top_of(0)
            parts(0, 0)

            def body(g, k, hp):
                def output(lp):
                    dve.wait_ge(pv_done, g * ST + 16 * lp + 16)
                    nc.vector.reciprocal(rec[:], pZ[:]).then_inc(dv2, 1)
                    dve.wait_ge(dv2, g * 2 + lp + 1)
                    if lp or at_least(g, 1):
                        dve.wait_ge(o_lo, g * 2 + lp)
                    nc.vector.tensor_tensor(o[:], pO[:], rec[:], ALU.mult).then_inc(o_read, 1)

                for step in range(ST):
                    if before(g, NG - 1):
                        maxima(g + 1, m_units(step))
                        if step == MBY - 1:
                            top_of(g + 1)
                        if step == ST - 1:
                            parts(g + 1, (k + 1) % U)
                    if step == 16:
                        output(0)
                output(1)
            groups(dve, body)

        @block.tensor
        def _(pe):
            def maxima(g, k, units):
                for n in units:
                    if n == 0:
                        pe.wait_ge(loaded[k], (g - k) * 24 + 96)
                    if n >= 3 or at_least(g, 1):
                        pe.wait_ge(m_read, g * (NM + 1) + (n - 2))
                    h, t, mc = n // 64, n // 4 % 16, n % 4
                    nc.tensor.matmul(pM[n % 3][:], qs[k][0:KD, h, t * P:(t + 1) * P], ks[k][0:KD, h, mc * 512:(mc + 1) * 512],
                                     start=True, stop=True).then_inc(m_done, 1)

            def top_of(g):
                pe.wait_ge(top_ready, g + 1)
                nc.tensor.transpose(pM[NM % 3][0:32, 0:P], top[:], ident[:]).then_inc(m_done, 1)

            pe.wait_ge(cleared, 2 + U)
            maxima(0, 0, range(NM))
            top_of(0)

            def body(g, k, hp):
                def scores(step, cs):
                    lp, mt = step // 16, step % 16
                    for c in cs:
                        n = 4 * step + c
                        h, lc = c // 2, 2 * lp + c % 2
                        if n >= 3 or at_least(g, 1):
                            pe.wait_ge(exp_done, g * 4 * ST + (n - 2 if n >= 3 else (-1, 0, -2)[n]))
                        nc.tensor.matmul(pS[n % 3][:], ks[k][:, h, mt * P:(mt + 1) * P], qs[k][:, h, lc * 512:(lc + 1) * 512],
                                         start=True, stop=True).then_inc(s_done, 1)

                def values(step):
                    lp, mt = step // 16, step % 16
                    pe.wait_ge(exp_done, g * 4 * ST + 4 * step + 4)
                    if mt == 0 and (lp or at_least(g, 1)):
                        pe.wait_ge(o_read, g * 2 + lp)
                    for c in range(4):
                        nc.tensor.matmul(pO[c * HD:(c + 1) * HD, :], V[k % 2][:, mt, (c // 2) * HD:(c // 2 + 1) * HD],
                                         prob[step % 4][:, c, :], start=mt == 0, stop=mt == 15, skip_group_check=True)

                def sums(step):
                    mt = step % 16
                    for c in range(4):
                        last = nc.tensor.matmul(pZ[c * HD:(c + 1) * HD, :], ones[:], prob[step % 4][:, c, :],
                                                start=mt == 0, stop=mt == 15, skip_group_check=True)
                    last.then_inc(pv_done, 1)

                pe.wait_ge(top_rows[k], (g - k) * 8 + 32)
                pe.wait_ge(v_loaded[k % 2], (g - k % 2) * 8 + 16)
                for step in range(ST):
                    units = list(m_units(step)) if before(g, NG - 1) else []
                    scores(step, (0, 1, 2))
                    if step:
                        values(step - 1)
                    scores(step, (3,))
                    maxima(g + 1, (k + 1) % U, units[:2])
                    if step:
                        sums(step - 1)
                    maxima(g + 1, (k + 1) % U, units[2:])
                    if step == ST - 1 and before(g, NG - 1):
                        top_of(g + 1)
                values(ST - 1)
                sums(ST - 1)
            groups(pe, body)


def proj_phase(nc, io, keep):
    with ExitStack() as ctx:
        m = Mem(nc, ctx, "prj")
        NCH = B * S // 512
        ident, modA, modB = keep["ident"], keep["modA"], keep["modB"]
        stage = m.sb("stage", [P, DC, D])
        W = m.sb("W", [P, 2, DC, D], F32R)
        bp = m.sb("bp", [P, D])
        gate = [m.sb(f"gate{i}", [P, D]) for i in range(2)]
        os_ = [m.sb(f"os{i}", [P, 2, DC, 512], F32R) for i in range(2)]
        xr = [m.sb(f"xr{i}", [P, 4, D]) for i in range(2)]
        x2 = [m.sb(f"x2{i}", [P, 4, D]) for i in range(2)]
        xn = m.sb("xn", [P, 4, D])
        th = [m.sb(f"th{i}", [P, 512]) for i in range(2)]
        hs = [m.sb(f"hs{i}", [P, 2, 512], F32R) for i in range(4)]
        stats, mv = m.sb("stats", [P, 4, 6]), m.sb("mv", [P, 4, 2])
        rstd, tmp = m.sb("rstd", [P, 4]), m.sb("tmp", [P, 12])
        pT = [m.ps(f"pT{i}") for i in range(4)]
        pp = [m.ps(f"pp{i}") for i in range(4)]

        w_loaded, b_loaded, w_hi, w_lo = [m.sem(x) for x in ("w_loaded", "b_loaded", "w_hi", "w_lo")]
        o_loaded, x_loaded, g_loaded = m.sems("o_loaded", 2), m.sems("x_loaded", 2), m.sems("g_loaded", 2)
        x_stored, h_stored = m.sems("x_stored", 2), m.sems("h_stored", 4)
        var_ready, root_ready, xn_ready, tr_done, h_hi, h_lo = [
            m.sem(x) for x in ("var_ready", "root_ready", "xn_ready", "tr_done", "h_hi", "h_lo")]
        p_done, p_read, x2_ready, dv, gated = [m.sem(x) for x in ("p_done", "p_read", "x2_ready", "dv", "gated")]
        block = m.block()

        @block.sync
        def _(sp):
            def load(i, s):
                at = bass.ds(i * 512, 512)
                for k in range(2):
                    sp.dma_start(raw(os_[s][:, k]), io["o_d"][k, :, at].rearrange("(c p) n -> p c n", p=P)).then_inc(o_loaded[s], 16)
                sp.dma_start(xr[s][:], io["x1_d"][at, :].rearrange("(n p) d -> p n d", p=P)).then_inc(x_loaded[s], 16)
                sp.dma_start(gate[s][:], io["gate_d"][0, bass.ds(i, 1)].rearrange("a p d -> (a p) d")).then_inc(g_loaded[s], 16)

            sp.dma_start(stage[:], io["Wproj"].rearrange("(c p) n -> p c n", p=P)).then_inc(w_loaded, 16)
            load(0, 0)
            sp.dma_start(bp[:], io["rows"][6:7, :].to_broadcast([P, D])).then_inc(b_loaded, 16)
            load(1, 1)

            def body(i, s):
                sp.wait_ge(x2_ready, i * 4 + 4)
                sp.dma_start(io["x2_d"][bass.ds(i * 512, 512), :].rearrange("(n p) d -> p n d", p=P), x2[s][:]).then_inc(x_stored[s], 16)
                if before(i, NCH - 2):
                    load(i + 2, s)
            tiles(sp, NCH, 2, body)
            for x in x_stored:
                sp.wait_ge(x, 16 * NCH // 2)
            for x in h_stored:
                sp.wait_ge(x, 16 * NCH)

        @block.scalar
        def _(act):
            act.wait_ge(w_loaded, 16)
            nc.scalar.activation(W[:, 0], stage[:], ACT.Identity).then_inc(w_hi, 1)

            def store(i, c):
                dst = io["h2_d"][:, c * P:(c + 1) * P, bass.ds(i * 512, 512)]
                act.dma_start(dst.rearrange("a p n -> p a n"), raw(hs[c][:])).then_inc(h_stored[c], 16)

            def body(i, s):
                act.wait_ge(var_ready, i + 1)
                nc.scalar.activation(tmp[:, 4:8], tmp[:, 0:4], ACT.Sqrt).then_inc(root_ready, 1)
                for c in range(DC):
                    if c >= 2:
                        act.wait_ge(h_lo, i * 4 + c - 1)
                        store(i, c - 2)
                    elif at_least(i, 1):
                        act.wait_ge(h_lo, i * 4 + c - 1)
                        store(i - 1, c + 2)
                    act.wait_ge(tr_done, i * 4 + c + 1)
                    if at_least(i, 1):
                        act.wait_ge(h_stored[c], i * 16)
                    a, b = modA[:, 1, bass.ds(i * DC + c, 1)], modB[:, 1, bass.ds(i * DC + c, 1)]
                    nc.scalar.activation(th[c % 2][:], pT[c][:], ACT.Identity, bias=b, scale=a)
                    nc.scalar.activation(hs[c][:, 0, :], pT[c][:], ACT.Identity, bias=b, scale=a).then_inc(h_hi, 1)
            tiles(act, NCH, 2, body)
            for c in (2, 3):
                act.wait_ge(h_lo, NCH * 4 - 3 + c)
                store(NCH - 1, c)

        @block.vector
        def _(dve):
            dve.wait_ge(w_hi, 1)
            nc.vector.tensor_tensor(W[:, 1], stage[:], W[:, 0], ALU.subtract).then_inc(w_lo, 1)
            dve.wait_ge(b_loaded, 16)

            def low(i, c):
                dve.wait_ge(h_hi, i * 4 + c + 1)
                nc.vector.tensor_tensor(hs[c][:, 1, :], th[c % 2][:], hs[c][:, 0, :], ALU.subtract).then_inc(h_lo, 1)

            def body(i, s):
                link = steps(dve, dv, i * NORM_LINKS)
                for nt in range(4):
                    n = i * 4 + nt
                    row = x2[s][:, nt, :]
                    if nt == 0 and at_least(i, 2):
                        dve.wait_ge(x_stored[s], (i - s) * 8)
                    dve.wait_ge(p_done, n + 1)
                    nc.vector.tensor_tensor(row, pp[nt][:], bp[:], ALU.add).then_inc(p_read, 1)
                    if nt == 0:
                        dve.wait_ge(x_loaded[s], (i - s) * 8 + 16)
                        dve.wait_ge(g_loaded[s], (i - s) * 8 + 16)
                    dve.wait_ge(p_read, n + 1)
                    nc.vector.tensor_tensor(row, row, gate[s][:], ALU.mult).then_inc(gated, 1)
                    dve.wait_ge(gated, n + 1)
                    nc.vector.tensor_tensor(row, row, xr[s][:, nt, :], ALU.add).then_inc(x2_ready, 1)
                    if at_least(i, 1):
                        low(i - 1, nt)
                dve.wait_ge(x2_ready, i * 4 + 4)
                norm_rows(nc, dve, link, x2[s], stats, mv, rstd, tmp, var_ready, root_ready, i)
                if at_least(i, 1):
                    dve.wait_ge(tr_done, i * 4)
                for nt in range(4):
                    last = nc.vector.tensor_scalar(xn[:, nt, :], x2[s][:, nt, :], mv[:, nt, 0:1], rstd[:, nt:nt + 1],
                                                   ALU.subtract, ALU.mult)
                last.then_inc(xn_ready, 1)
            tiles(dve, NCH, 2, body)
            for c in range(DC):
                low(NCH - 1, c)

        @block.tensor
        def _(pe):
            def project(i, s):
                pe.wait_ge(o_loaded[s], (i - s) * 16 + 32)
                for nt in range(4):
                    if at_least(i, 1):
                        pe.wait_ge(p_read, i * 4 + nt - 3)
                    for n, (k, w) in enumerate(PASSES):
                        for c in range(DC):
                            last = nc.tensor.matmul(pp[nt][:], os_[s][:, k, c, nt * P:(nt + 1) * P], W[:, w, c, :],
                                                    start=n + c == 0, stop=n == 2 and c == DC - 1)
                    last.then_inc(p_done, 1)

            pe.wait_ge(w_lo, 1)
            project(0, 0)

            def body(i, s):
                if before(i, NCH - 1):
                    project(i + 1, 1 - s)
                pe.wait_ge(xn_ready, i + 1)
                for c in range(DC):
                    if at_least(i, 1):
                        pe.wait_ge(h_hi, i * 4 + c - 3)
                    for nt in range(4):
                        last = nc.tensor.transpose(pT[c][:, nt * P:(nt + 1) * P], xn[:, nt, c * P:(c + 1) * P], ident[:])
                    last.then_inc(tr_done, 1)
            tiles(pe, NCH, 2, body)


def mlp_phase(nc, io, keep):
    with ExitStack() as ctx:
        m = Mem(nc, ctx, "mlp")
        NCH = B * S // 512
        cols = keep["cols"]
        W1 = m.sb("W1", [P, 2, DC, MLP], F32R)
        W2 = m.sb("W2", [P, 2, MC, D], F32R)
        b2 = m.sb("b2", [P, D])
        gate = [m.sb(f"gate{i}", [P, D]) for i in range(2)]
        hs = [m.sb(f"hs{i}", [P, 2, DC, 512], F32R) for i in range(2)]
        xr = [m.sb(f"xr{i}", [P, 4, D]) for i in range(2)]
        tu = [m.sb(f"tu{i}", [P, 512]) for i in range(2)]
        us = [m.sb(f"us{i}", [P, 2, 512], F32R) for i in range(2)]
        y = [m.sb(f"y{i}", [P, D]) for i in range(4)]
        pu = [m.ps(f"pu{i}") for i in range(4)]
        pa = [m.ps(f"pa{i}") for i in range(4)]

        w_loaded, b_loaded, w_hi, w_lo = m.sems("w_loaded", 2), m.sem("b_loaded"), m.sem("w_hi"), m.sem("w_lo")
        h_loaded, x_loaded, g_loaded, stored = m.sems("h_loaded", 2), m.sems("x_loaded", 2), m.sems("g_loaded", 2), m.sems("stored", 4)
        u_done, u_hi, u_lo, u_used, a_done, a_read, gated, y_ready = [
            m.sem(x) for x in ("u_done", "u_hi", "u_lo", "u_used", "a_done", "a_read", "gated", "y_ready")]
        block = m.block()
        NP = 8

        def piece(n):
            if n < DC:
                return lambda k: W1[:, k, n, :].rearrange("p (a b) -> p a b", a=4)
            return lambda k: W2[:, k, (n - DC) * 4:(n - DC + 1) * 4, :]

        @block.sync
        def _(sp):
            def load_h(i, s):
                at = bass.ds(i * 512, 512)
                for k in range(2):
                    sp.dma_start(raw(hs[s][:, k]), io["h2_d"][k, :, at].rearrange("(c p) n -> p c n", p=P)).then_inc(h_loaded[s], 16)

            def load_x(i, s):
                at = bass.ds(i * 512, 512)
                sp.dma_start(xr[s][:], io["x2_d"][at, :].rearrange("(n p) d -> p n d", p=P)).then_inc(x_loaded[s], 16)
                sp.dma_start(gate[s][:], io["gate_d"][1, bass.ds(i, 1)].rearrange("a p d -> (a p) d")).then_inc(g_loaded[s], 16)

            for n in range(NP):
                if n >= 2:
                    sp.wait_ge(w_lo, n - 1)
                if n < DC:
                    src = io["W1"][n * P:(n + 1) * P, :].rearrange("p (a b) -> p a b", a=4)
                else:
                    src = io["W2"][(n - DC) * 512:(n - DC + 1) * 512, :].rearrange("(a p) d -> p a d", p=P)
                sp.dma_start(xr[n % 2][:], src).then_inc(w_loaded[n % 2], 16)
                if n == 1:
                    load_h(0, 0)
                    sp.dma_start(b2[:], io["rows"][7:8, :].to_broadcast([P, D])).then_inc(b_loaded, 16)
            load_h(1, 1)
            sp.wait_ge(w_lo, NP)
            load_x(0, 0)
            load_x(1, 1)

            def body(i, s):
                if before(i, NCH - 2):
                    sp.wait_ge(u_done, i * MC + MC)
                    load_h(i + 2, s)
                for nt in range(4):
                    sp.wait_ge(y_ready, i * 4 + nt + 1)
                    sp.dma_start(io["out"][bass.ds(i * 512 + nt * P, P), :], y[nt][:]).then_inc(stored[nt], 16)
                if before(i, NCH - 2):
                    load_x(i + 2, s)
            tiles(sp, NCH, 2, body)
            for x in stored:
                sp.wait_ge(x, 16 * NCH)

        @block.scalar
        def _(act):
            for n in range(NP):
                act.wait_ge(w_loaded[n % 2], 16 * (n // 2 + 1))
                nc.scalar.activation(piece(n)(0), xr[n % 2][:], ACT.Identity).then_inc(w_hi, 1)

            def body(i, s):
                for j in range(MC):
                    n = i * MC + j
                    act.wait_ge(u_done, n + 1)
                    if j >= 2 or at_least(i, 1):
                        act.wait_ge(u_lo, n - 1)
                    if j >= 2:
                        act.wait_ge(u_used, i * (MC - 1) + j - 1)
                    elif j == 1 and at_least(i, 1):
                        act.wait_ge(a_done, i * 4)
                    elif at_least(i, 1):
                        act.wait_ge(u_used, i * (MC - 1))
                    bias = cols[:, COLS["b1"][0] + j:COLS["b1"][0] + j + 1]
                    nc.scalar.activation(tu[j % 2][:], pu[j % 4][:], ACT.Gelu, bias=bias)
                    nc.scalar.activation(us[j % 2][:, 0, :], pu[j % 4][:], ACT.Gelu, bias=bias).then_inc(u_hi, 1)
            tiles(act, NCH, 2, body)

        @block.vector
        def _(dve):
            for n in range(NP):
                dve.wait_ge(w_hi, n + 1)
                nc.vector.tensor_tensor(piece(n)(1), xr[n % 2][:], piece(n)(0), ALU.subtract).then_inc(w_lo, 1)
            dve.wait_ge(b_loaded, 16)

            def low(n, j):
                dve.wait_ge(u_hi, n + 1)
                nc.vector.tensor_tensor(us[j % 2][:, 1, :], tu[j % 2][:], us[j % 2][:, 0, :], ALU.subtract).then_inc(u_lo, 1)

            def outputs(i, s):
                dve.wait_ge(x_loaded[s], (i - s) * 8 + 16)
                dve.wait_ge(g_loaded[s], (i - s) * 8 + 16)
                for nt in range(4):
                    dve.wait_ge(a_done, i * 4 + nt + 1)
                    if at_least(i, 1):
                        dve.wait_ge(stored[nt], i * 16)
                    nc.vector.tensor_tensor(y[nt][:], pa[nt][:], b2[:], ALU.add).then_inc(a_read, 1)
                for nt in range(4):
                    dve.wait_ge(a_read, i * 4 + nt + 1)
                    nc.vector.tensor_tensor(y[nt][:], y[nt][:], gate[s][:], ALU.mult).then_inc(gated, 1)
                for nt in range(4):
                    dve.wait_ge(gated, i * 4 + nt + 1)
                    nc.vector.tensor_tensor(y[nt][:], y[nt][:], xr[s][:, nt, :], ALU.add).then_inc(y_ready, 1)

            low(0, 0)

            def body(i, s):
                for j in range(1, MC):
                    low(i * MC + j, j)
                if before(i, NCH - 1):
                    low((i + 1) * MC, 0)
                outputs(i, s)
            tiles(dve, NCH, 2, body)

        @block.tensor
        def _(pe):
            def hidden(i, s, j):
                n = i * MC + j
                if j == 0:
                    pe.wait_ge(h_loaded[s], (i - s) * 16 + 32)
                if j >= 4 or at_least(i, 1):
                    pe.wait_ge(u_hi, n - 3)
                for q, (k, w) in enumerate(PASSES):
                    for c in range(DC):
                        last = nc.tensor.matmul(pu[j % 4][:], W1[:, k, c, j * P:(j + 1) * P], hs[s][:, w, c, :],
                                                start=q + c == 0, stop=q == 2 and c == DC - 1)
                last.then_inc(u_done, 1)

            pe.wait_ge(w_lo, DC)
            hidden(0, 0, 0)

            def body(i, s):
                for j in range(MC):
                    if j < MC - 1:
                        hidden(i, s, j + 1)
                    elif before(i, NCH - 1):
                        hidden(i + 1, 1 - s, 0)
                    if isinstance(i, int) and i == 0 and j % 4 == 0:
                        pe.wait_ge(w_lo, DC + 1 + j // 4)
                    pe.wait_ge(u_lo, i * MC + j + 1)
                    for nt in range(4):
                        if j == 0 and at_least(i, 1):
                            pe.wait_ge(a_read, i * 4 + nt - 3)
                        for q, (k, w) in enumerate(PASSES):
                            last = nc.tensor.matmul(pa[nt][:], us[j % 2][:, k, nt * P:(nt + 1) * P], W2[:, w, j, :],
                                                    start=j + q == 0, stop=j == MC - 1 and q == 2)
                        if j == MC - 1:
                            last.then_inc(a_done, 1)
                    if j < MC - 1:
                        last.then_inc(u_used, 1)
            tiles(pe, NCH, 2, body)


def build(nc, io, upto=9):
    for name, shape, dt in [("x1_d", (B * S, D), F32), ("gate_d", (2, B * S // 512, P, D), F32),
                            ("qk_d", (2, 2, D, B * S), F32), ("v_d", (B * S, D), F32),
                            ("o_d", (2, D, B * S), F32), ("x2_d", (B * S, D), F32), ("h2_d", (2, D, B * S), F32)]:
        io[name] = nc.dram_tensor(name, shape, dt, kind="Internal").ap()
    with ExitStack() as ctx:
        m = Mem(nc, ctx, "keep")
        keep = {"cols": m.sb("cols", [P, NCOLS]), "ident": m.sb("ident", [P, P]),
                "modA": m.sb("modA", [P, 2, B * S // 512 * DC]), "modB": m.sb("modB", [P, 2, B * S // 512 * DC])}
        with ExitStack() as early:
            e = Mem(nc, early, "graph")
            keep["floor4"] = e.sb("floor4", [4, 1])
            keep["wl_bc"] = e.sb("wl_bc", [P, 2 * NONGT * L])
            keep["bb"] = e.sb("bb", [P, 1])
            keep["LW"] = e.sb("LW", [P, 2, B, DC, D + 2 * HM], F32R)
            keep["VB"] = e.sb("VB", [GM, B, 2, DC, P])
            keep["r4"] = e.sb("r4", [4, B, D + 2 * HM], F32R)
            setup_phase(nc, io, keep)
            graph_phase(nc, io, keep)
        if upto > 1:
            qkv_phase(nc, io, keep)
        if upto > 2:
            attention_phase(nc, io, keep)
        if upto > 3:
            proj_phase(nc, io, keep)
        if upto > 4:
            mlp_phase(nc, io, keep)


_OUT = [((B, S, D), "float32")]


def layouts(inp):
    a = {k: np.asarray(v) for k, v in inp.items()}
    x, mask = a["x"], a["mask_BxSxSx11_ik0"]

    def columns(v):
        return np.ascontiguousarray(v.reshape(-1, P).T)
    bqkv, bt = a["L1_cond_bqkv"], a["L1_cond_bt"]
    cols = np.concatenate([
        a["cond_1024"].reshape(B, DC, P).transpose(2, 1, 0).reshape(P, DC * B), columns(a["L0_cond_b_self"]),
        columns(a["L0_cond_bq"]), columns(a["L0_cond_bk"]), columns(bqkv[:2 * D]),
        columns(a["L1_cond_g1"]), columns(a["L1_cond_g2"]), columns(a["L1_cond_be1"]), columns(a["L1_cond_be2"]),
        columns(a["L1_cond_b1"]), columns(bt)], axis=1)
    rows = np.stack([a["L0_cond_b_self"], a["L0_cond_bout"][0], a["L0_cond_bout"][1], bt[2 * D:3 * D], bt[5 * D:6 * D],
                     bqkv[2 * D:], a["L1_cond_bproj"], a["L1_cond_b2"]])
    near = np.stack([mask[:, :, :NONGT, :], mask[:, :NONGT, :, :].swapaxes(1, 2)], axis=2)
    wl = np.concatenate([np.tile(a["L0_cond_w_bias"], 2 * NONGT), a["L0_cond_b_bias"].reshape(1)])[None]
    out = {
        "x": x.reshape(B * S, D), "xT": x.transpose(0, 2, 1), "mask": near.reshape(B * S, 2 * NONGT * L),
        "cols": cols, "rows": rows, "wl": wl,
        "ident": np.eye(P, dtype=np.float32), "floor4": np.array([[0], [0], [1], [1]], np.float32),
        "Wself": a["L0_cond_W_self"], "WselfT": a["L0_cond_W_self"].T,
        "Wq": a["L0_cond_Wq"], "WkT": a["L0_cond_Wk"].transpose(0, 2, 1),
        "WoutT": a["L0_cond_Wout"].reshape(2, D, D).transpose(0, 2, 1),
        "Wqkv": a["L1_cond_Wqkv"], "Wproj": a["L1_cond_Wproj"], "W1": a["L1_cond_W1"], "W2": a["L1_cond_W2"], "Wt": a["L1_cond_Wt"],
    }
    return {k: np.ascontiguousarray(v) for k, v in out.items()}


def kernel(**inputs):
    import concourse.bacc as bacc
    from concourse.bass_utils import run_bass_kernel_spmd

    nc = bacc.Bacc("TRN2", target_bir_lowering=False, num_devices=1)
    arrays = layouts(inputs)
    io = {k: nc.dram_tensor(f"in_{k}", v.shape, mybir.dt.from_np(v.dtype), kind="ExternalInput").ap() for k, v in arrays.items()}
    io["out"] = nc.dram_tensor("out", (B * S, D), F32, kind="ExternalOutput").ap()
    build(nc, io)
    r = run_bass_kernel_spmd(nc, [{f"in_{k}": v for k, v in arrays.items()}], core_ids=[0])
    return r.results[0]["out"].reshape(B, S, D)
```

```python
import concourse.bass as bass
from concourse import mybir
from contextlib import ExitStack
import numpy as np

F32 = mybir.dt.float32
F32R = mybir.dt.float32r
I32 = mybir.dt.int32
ALU = mybir.AluOpType
ACT = mybir.ActivationFunctionType
AX = mybir.AxisListType

P = 128
B = 2
S = 2048
D = 512
DC = D // P
H = 16
HD = D // H
NONGT = 20
L = 11
HM = H * NONGT
HPC = P // HD
GM = HPC * NONGT
MLP = 4 * D
MC = MLP // P
NEG = -9000000000000000.0
SCALE = float(1.0 / np.sqrt(HD))
EPS = 1e-5
LO_HI = 2
PASSES = [(0, 0), (0, 1), (1, 0)]

COLS = {}
_at = 0
for _name, _n in [("cond", B * DC), ("b_self", DC), ("bq", 2 * DC), ("bk", 2 * DC), ("bqk", 2 * DC),
                  ("g", 2 * DC), ("be", 2 * DC), ("b1", MC), ("bt", 6 * DC)]:
    COLS[_name] = (_at, _n)
    _at += _n
NCOLS = _at
ROWS = ["b_self", "bout0", "bout1", "bt_gate_msa", "bt_gate_mlp", "bv", "bproj", "b2"]


def tiles(eng, n, unroll, body):
    for t in range(unroll):
        body(t, t)
    if n > 2 * unroll:
        with eng.Fori(1, n // unroll - 1) as i:
            for k in range(unroll):
                body(i * unroll + k, k)
    for t in range(max(n - unroll, unroll), n):
        body(t, t % unroll)


def at_least(t, n):
    return not isinstance(t, int) or t >= n


def before(t, n):
    return not isinstance(t, int) or t < n


def steps(eng, sem, first=0):
    count = [0]

    def link(ins):
        count[0] += 1
        ins.then_inc(sem, 1)
        eng.wait_ge(sem, first + count[0])
    return link


def raw(ap):
    return ap.bitcast(F32)


class Mem:

    def __init__(self, nc, ctx, tag):
        self.nc, self.ctx, self.tag, self.used = nc, ctx, tag, []

    def sb(self, name, shape, dt=F32):
        return self.ctx.enter_context(self.nc.sbuf_tensor(f"{self.tag}_{name}", shape, dt))

    def ps(self, name, shape=(P, 512), dt=F32):
        return self.ctx.enter_context(self.nc.psum_tensor(f"{self.tag}_{name}", list(shape), dt))

    def sem(self, name):
        self.used.append(self.nc.alloc_semaphore(f"{self.tag}_{name}"))
        return self.used[-1]

    def block(self):
        self.ctx.callback(self.retire)
        return self.ctx.enter_context(self.nc.Block())

    def retire(self):
        self.nc.clear_and_free_semaphores(self.used)
        self.nc.all_engine_barrier()

    def sems(self, name, n):
        return [self.sem(f"{name}{i}") for i in range(n)]


def setup_phase(nc, io, keep):
    with ExitStack() as ctx:
        m = Mem(nc, ctx, "set")
        NB = S // 512
        cols, ident = keep["cols"], keep["ident"]
        WsT = m.sb("WsT", [P, 2 * DC, D])
        Wsn = m.sb("Wsn", [P, DC, D])
        WkT_Gs = m.sb("WkT_Gs", [P, 2 * DC * B * HM])
        WkT = WkT_Gs[:, 0:2 * DC * D].rearrange("p (d c n) -> p d c n", d=2, c=DC)
        Gs = WkT_Gs[:].rearrange("p (d c b g) -> p d c b g", d=2, c=DC, b=B)
        Wq = m.sb("Wq", [P, 2, DC, D])
        WoT = Wq
        Wt = [m.sb(f"Wt{i}", [P, DC, D]) for i in range(2)]
        xT20 = m.sb("xT20", [P, DC, B, NONGT])
        e_cond = m.sb("e_cond", [P, DC * B])
        silu = m.sb("silu", [P, DC, B])
        silu_bc = m.sb("silu_bc", [P, B, DC, P])
        gate_b = m.sb("gate_b", [P, 2, D])
        gate0 = m.sb("gate0", [P, 2, D])
        tp = m.sb("tp", [P, 4 * DC, B])
        scale1 = m.sb("scale1", [P, 2, B, DC])
        moda, modb = m.sb("moda", [P, 2, B, DC]), m.sb("modb", [P, 2, B, DC])
        cq = m.sb("cq", [P, DC, B])
        qnz = m.sb("qnz", [P, DC, B, NONGT])
        sf20 = m.sb("sf20", [P, DC, B * NONGT])
        ones = m.sb("ones", [P, P])
        kt = m.sb("kt", [P, 2, DC, B * NONGT])
        Kblk = m.sb("Kblk", [P, 2, DC, B, GM])
        rows_in = m.sb("rows_in", [3, D])
        row = m.sb("row", [P, D + 2 * HM])
        row_parts = m.sb("row_parts", [P, 2, D + 2 * HM], F32R)
        vp = m.sb("vp", [P, D])
        pb = [m.ps(f"pb{i}") for i in range(8)]

        ld_small, ld_w, ld_k, ld_q, ld_o = [m.sem(x) for x in ("ld_small", "ld_w", "ld_k", "ld_q", "ld_o")]
        ld_t = m.sems("ld_t", 2)
        st = m.sem("st")
        e_ready, silu_ready, bc_ready, cleared = [m.sem(x) for x in ("e_ready", "silu_ready", "bc_ready", "cleared")]
        piece_done, gate_done, gate_ready = [m.sem(x) for x in ("piece_done", "gate_done", "gate_ready")]
        cq_done, cq_ready, sf_done, sf_ready = [m.sem(x) for x in ("cq_done", "cq_ready", "sf_done", "sf_ready")]
        kt_done, K_ready, G_done, G_ready = [m.sem(x) for x in ("kt_done", "K_ready", "G_done", "G_ready")]
        row_done, row_ready, parts_ready = [m.sem(x) for x in ("row_done", "row_ready", "parts_ready")]
        h_done, h_hi, h_lo, vp_done, vp_ready = [m.sem(x) for x in ("h_done", "h_hi", "h_lo", "vp_done", "vp_ready")]
        dv = m.sem("dv")
        w1_ready = m.sem("w1_ready")
        block = m.block()
        LW, VB, r4 = keep["LW"], keep["VB"], keep["r4"]

        def col(name, i=0, n=1):
            at = COLS[name][0] + i
            return cols[:, at:at + n]

        cond_v = col("cond", 0, B * DC).rearrange("p (c b) -> p c b", b=B)
        bt = COLS["bt"][0]
        tp_chunks = [0, 1, 2, 3, 4, 5, 6, 7, 12, 13, 14, 15, 16, 17, 18, 19]

        @block.sync
        def _(sp):
            sp.dma_start(cols[:], io["cols"]).then_inc(ld_small, 16)
            sp.dma_start(ident[:], io["ident"]).then_inc(ld_small, 16)
            sp.dma_start(keep["floor4"][:], io["floor4"]).then_inc(ld_small, 16)
            sp.dma_start(keep["wl_bc"][:], io["wl"][0:1, 0:2 * NONGT * L].to_broadcast([P, 2 * NONGT * L])).then_inc(ld_small, 16)
            sp.dma_start(keep["bb"][:], io["wl"][0:1, 2 * NONGT * L:2 * NONGT * L + 1].to_broadcast([P, 1])).then_inc(ld_small, 16)
            sp.dma_start(rows_in[:], io["rows"][0:3, :]).then_inc(ld_small, 16)
            for k in range(2):
                sp.dma_start(gate_b[:, k, :], io["rows"][3 + k:4 + k, :].to_broadcast([P, D])).then_inc(ld_small, 16)
            sp.dma_start(WsT[:], io["WselfT"].rearrange("(c p) n -> p c n", p=P)).then_inc(ld_w, 16)
            for b in range(B):
                sp.dma_start(xT20[:, :, b, :], io["xT"][b, :, 0:NONGT].rearrange("(c p) n -> p c n", p=P)).then_inc(ld_w, 16)
            wt_v = io["Wt"].rearrange("(c p) n -> p c n", p=P)
            for n in range(2):
                sp.dma_start(Wt[n][:], wt_v[:, :, n * D:(n + 1) * D]).then_inc(ld_t[n], 16)
            sp.dma_start(WkT, io["WkT"].rearrange("d (c p) n -> p d c n", p=P)).then_inc(ld_k, 16)
            sp.dma_start(Wq[:], io["Wq"].rearrange("d (c p) n -> p d c n", p=P)).then_inc(ld_q, 16)
            sp.dma_start(Wsn[:], io["Wself"][:, 0:D].rearrange("(c p) n -> p c n", p=P)).then_inc(ld_q, 16)
            for n in range(2, 6):
                sp.wait_ge(piece_done, n - 1)
                sp.dma_start(Wt[n % 2][:], wt_v[:, :, n * D:(n + 1) * D]).then_inc(ld_t[n % 2], 16)
            sp.wait_ge(G_done, 16)
            sp.dma_start(WoT[:], io["WoutT"].rearrange("d (c p) n -> p d c n", p=P)).then_inc(ld_o, 16)
            sp.wait_ge(gate_ready, 4)
            for k in range(2):
                for b in range(B):
                    for n in range(b * NB, (b + 1) * NB):
                        sp.dma_start(io["gate_d"][k, n], (gate_b if b else gate0)[:, k, :]).then_inc(st, 16)
            sp.wait_ge(parts_ready, 1)
            for b in range(B):
                for k in range(2):
                    for h in range(2):
                        at = 32 * (2 * k + b)
                        sp.dma_start(raw(r4[2 * k + h:2 * k + h + 1, b, :]), raw(row_parts[at:at + 1, h, :])).then_inc(st, 16)
            sp.wait_ge(cleared, 3)
            for b in range(B):
                for d in range(2):
                    sp.wait_ge(vp_ready, 2 * b + d + 1)
                    for r in range(HPC):
                        dst = VB[r * NONGT:(r + 1) * NONGT, b, d, :, r * HD:(r + 1) * HD]
                        at = 32 * (2 * b + d)
                        src = vp[at:at + NONGT, :].rearrange("p (j q) -> p j q", q=P)[:, :, r * HD:(r + 1) * HD]
                        sp.dma_start(dst, src).then_inc(st, 16)
            sp.wait_ge(st, 16 * (4 * NB + 8 + 16))

        @block.scalar
        def _(act):
            act.wait_ge(ld_small, 16 * 8)
            nc.scalar.activation(e_cond[:], col("cond", 0, B * DC), ACT.Exp, scale=-1.0).then_inc(e_ready, 1)
            for n in range(4):
                act.wait_ge(vp_done, n + 1)
                nc.scalar.activation(vp[32 * n:32 * n + NONGT, :], pb[2 + n % 2][32 * n:32 * n + NONGT, :], ACT.Identity).then_inc(vp_ready, 1)
            n = 0
            for b in range(B):
                for d in range(2):
                    for ic in range(DC):
                        act.wait_ge(h_done, n + 1)
                        nc.scalar.activation(LW[:, 0, b, ic, D + d * HM:D + (d + 1) * HM], pb[n % 2][:, 0:HM],
                                             ACT.Identity).then_inc(h_hi, 1)
                        n += 1

        @block.gpsimd
        def _(pool):
            nc.gpsimd.memset(VB[:], 0.0).then_inc(cleared, 1)
            nc.gpsimd.memset(Kblk[:], 0.0).then_inc(cleared, 1)
            nc.gpsimd.memset(ones[:], 1.0).then_inc(cleared, 1)
            pool.wait_ge(ld_w, 16 * 3)
            for b in range(B):
                nc.gpsimd.tensor_copy(LW[:, 0, b, :, 0:D], WsT[:, 0:DC, :]).then_inc(w1_ready, 1)
            for b in range(B):
                pool.wait_ge(w1_ready, B)
                nc.gpsimd.tensor_tensor(LW[:, 1, b, :, 0:D], WsT[:, 0:DC, :], LW[:, 0, b, :, 0:D], ALU.subtract).then_inc(w1_ready, 1)

        @block.vector
        def _(dve):
            link = steps(dve, dv)
            dve.wait_ge(ld_small, 16 * 8)
            dve.wait_ge(e_ready, 1)
            link(nc.vector.tensor_scalar_add(e_cond[:], e_cond[:], 1.0))
            link(nc.vector.reciprocal(e_cond[:], e_cond[:]))
            nc.vector.tensor_tensor(silu[:], cond_v, e_cond[:].rearrange("p (c b) -> p c b", b=B), ALU.mult).then_inc(silu_ready, 1)
            dve.wait_ge(silu_ready, 1)
            for b in range(B):
                nc.vector.tensor_copy(silu_bc[:, b], silu[:, :, b:b + 1].to_broadcast([P, DC, P])).then_inc(bc_ready, 1)
            dve.wait_ge(cq_done, 1)
            nc.vector.tensor_copy(cq[:], pb[0][:, 0:DC * B].rearrange("p (j b) -> p j b", b=B)).then_inc(cq_ready, 1)
            dve.wait_ge(cq_ready, 1)
            dve.wait_ge(sf_done, 1)
            for j in range(DC):
                for b in range(B):
                    last = nc.vector.tensor_scalar(qnz[:, j, b, :], pb[2][:, b * NONGT:(b + 1) * NONGT], 0.0,
                                                   cq[:, j, b:b + 1], ALU.not_equal, ALU.mult)
            link(last)
            for j in range(DC):
                last = nc.vector.scalar_tensor_tensor(sf20[:, j, :], pb[1][:, j * 40:(j + 1) * 40], col("b_self", j),
                                                      qnz[:, j].rearrange("p b m -> p (b m)"), ALU.add, ALU.add)
            last.then_inc(sf_ready, 1)
            dve.wait_ge(kt_done, 1)
            for d in range(2):
                for j in range(DC):
                    last = nc.vector.tensor_scalar(kt[:, d, j, :], pb[3][:, (d * DC + j) * 40:(d * DC + j + 1) * 40],
                                                   col("bk", d * DC + j), SCALE, ALU.add, ALU.mult)
            link(last)
            dve.wait_ge(cleared, 3)
            for r in range(HPC):
                dst = Kblk[r * HD:(r + 1) * HD, :, :, :, r * NONGT:(r + 1) * NONGT].rearrange("p d j b m -> p (d j) b m")
                src = kt[r * HD:(r + 1) * HD].rearrange("p d j (b m) -> p (d j) b m", m=NONGT)
                last = nc.vector.tensor_copy(dst, src)
            last.then_inc(K_ready, 1)
            for n in range(16):
                d, fc, half = n // 8, n // 2 % 4, n % 2
                dve.wait_ge(G_done, n + 1)
                dst = Gs[:, d, fc].rearrange("p b (j g) -> p j b g", g=GM)[:, 2 * half:2 * half + 2]
                src = pb[4 + n % 2][:, 0:4 * GM].rearrange("p (j b g) -> p j b g", j=2, b=B)
                nc.vector.tensor_copy(dst, src).then_inc(G_ready, 1)
            dve.wait_ge(piece_done, 2)
            dve.wait_ge(gate_done, 1)
            nc.vector.tensor_tensor(gate0[:, 0, :], pb[3][:], gate_b[:, 0, :], ALU.add).then_inc(gate_ready, 1)
            dve.wait_ge(piece_done, 3)
            nc.vector.tensor_tensor(gate_b[:, 0, :], pb[7][:], gate_b[:, 0, :], ALU.add).then_inc(gate_ready, 1)
            dve.wait_ge(piece_done, 5)
            for n, ch in enumerate(tp_chunks):
                last = nc.vector.tensor_scalar(tp[:, n, :], pb[6][:, n * B:(n + 1) * B], cols[:, bt + ch:bt + ch + 1], None, ALU.add)
            link(last)
            def per_chunk(ap):
                return ap.unsqueeze(2).to_broadcast([P, B, S // 512, DC])

            for k in range(2):
                g = col("g", k * DC, DC).unsqueeze(1).to_broadcast([P, B, DC])
                be = col("be", k * DC, DC).unsqueeze(1).to_broadcast([P, B, DC])
                shift = tp[:, 8 * k:8 * k + DC, :].rearrange("p c b -> p b c")
                scale = tp[:, 8 * k + DC:8 * k + 2 * DC, :].rearrange("p c b -> p b c")
                link(nc.vector.tensor_scalar_add(scale1[:, k], scale, 1.0))
                link(nc.vector.tensor_tensor(moda[:, k], scale1[:, k], g, ALU.mult))
                link(nc.vector.tensor_tensor(modb[:, k], scale1[:, k], be, ALU.mult))
                link(nc.vector.tensor_tensor(modb[:, k], modb[:, k], shift, ALU.add))
                for full, small in ((keep["modA"], moda), (keep["modB"], modb)):
                    nc.vector.tensor_copy(full[:, k].rearrange("p (b n c) -> p b n c", b=B, c=DC), per_chunk(small[:, k]))
            dve.wait_ge(gate_done, 2)
            nc.vector.tensor_tensor(gate0[:, 1, :], pb[3][:], gate_b[:, 1, :], ALU.add).then_inc(gate_ready, 1)
            dve.wait_ge(piece_done, 6)
            nc.vector.tensor_tensor(gate_b[:, 1, :], pb[7][:], gate_b[:, 1, :], ALU.add).then_inc(gate_ready, 1)
            for b in range(B):
                dve.wait_ge(row_done, 6 * b + 6)
                q, e = slice(32 * b, 32 * b + 1), slice(64 + 32 * b, 64 + 32 * b + 1)
                nc.vector.tensor_copy(row[q, 0:D], pb[0][q, :])
                nc.vector.tensor_copy(row[e, 0:D], pb[3][e, :])
                for d in range(2):
                    at = slice(D + d * HM, D + (d + 1) * HM)
                    nc.vector.tensor_copy(row[q, at], pb[1 + d][q, 0:HM])
                    last = nc.vector.tensor_copy(row[e, at], pb[4 + d][e, 0:HM])
                last.then_inc(row_ready, 1)
            dve.wait_ge(row_ready, 2)
            for k in range(4):
                at = slice(32 * k, 32 * k + 1)
                last = nc.vector.tensor_copy(row_parts[at, 0, :], row[at, :])
            link(last)
            for k in range(4):
                at = slice(32 * k, 32 * k + 1)
                last = nc.vector.tensor_tensor(row_parts[at, 1, :], row[at, :], row_parts[at, 0, :], ALU.subtract)
            last.then_inc(parts_ready, 1)
            n = 0
            for b in range(B):
                for d in range(2):
                    for ic in range(DC):
                        dve.wait_ge(h_hi, n + 1)
                        at = slice(D + d * HM, D + (d + 1) * HM)
                        nc.vector.tensor_tensor(LW[:, 1, b, ic, at], pb[n % 2][:, 0:HM], LW[:, 0, b, ic, at], ALU.subtract).then_inc(h_lo, 1)
                        n += 1

        @block.tensor
        def _(pe):
            def mm(out, a, b, first, last):
                return nc.tensor.matmul(out, a, b, start=first, stop=last)

            pe.wait_ge(ld_small, 16 * 8)
            pe.wait_ge(ld_w, 16 * 3)
            for j in range(DC):
                for c in range(DC):
                    last = mm(pb[0][:, j * B:(j + 1) * B], WsT[:, DC + c, j * P:(j + 1) * P], cond_v[:, c, :], c == 0, c == DC - 1)
            last.then_inc(cq_done, 1)
            for j in range(DC):
                for c in range(DC):
                    mm(pb[1][:, j * 40:(j + 1) * 40], WsT[:, c, j * P:(j + 1) * P],
                       xT20[:, c].rearrange("p b m -> p (b m)"), c == 0, c == DC - 1)
            pe.wait_ge(cleared, 3)
            for c in range(DC):
                last = mm(pb[2][:, 0:40], ones[:], xT20[:, c].rearrange("p b m -> p (b m)"), c == 0, c == DC - 1)
            last.then_inc(sf_done, 1)
            def modulation():
                pe.wait_ge(silu_ready, 1)
                pe.wait_ge(bc_ready, 2)
                for n in range(6):
                    pe.wait_ge(ld_t[n % 2], 16 * (n // 2 + 1))
                    if n % 3 < 2:
                        for j in range(DC):
                            at = (n - n // 3) * DC + j
                            for c in range(DC):
                                last = mm(pb[6][:, at * B:(at + 1) * B], Wt[n % 2][:, c, j * P:(j + 1) * P],
                                          silu[:, c, :], c == 0, c == DC - 1)
                        last.then_inc(piece_done, 1)
                    else:
                        if n == 5:
                            pe.wait_ge(gate_ready, 2)
                        for b in range(B):
                            for c in range(DC):
                                last = mm(pb[7 if b else 3][:], silu_bc[:, b, c, :], Wt[n % 2][:, c, :], c == 0, c == DC - 1)
                            if b == 0:
                                last.then_inc(gate_done, 1)
                        last.then_inc(piece_done, 1)

            pe.wait_ge(ld_k, 16)
            pe.wait_ge(sf_ready, 1)
            for d in range(2):
                for j in range(DC):
                    for c in range(DC):
                        last = mm(pb[3][:, (d * DC + j) * 40:(d * DC + j + 1) * 40], WkT[:, d, c, j * P:(j + 1) * P],
                                  sf20[:, c, :], c == 0, c == DC - 1)
            last.then_inc(kt_done, 1)
            pe.wait_ge(ld_q, 32)
            pe.wait_ge(K_ready, 1)
            for n in range(16):
                d, fc, half = n // 8, n // 2 % 4, n % 2
                if n >= 2:
                    pe.wait_ge(G_ready, n - 1)
                for k in range(2):
                    j = 2 * half + k
                    last = mm(pb[4 + n % 2][:, k * 2 * GM:(k + 1) * 2 * GM], Wq[:, d, j, fc * P:(fc + 1) * P],
                              Kblk[:, d, j].rearrange("p b g -> p (b g)"), True, True)
                last.then_inc(G_done, 1)
            modulation()
            pe.wait_ge(G_ready, 16)
            pe.wait_ge(cq_ready, 1)
            pe.wait_ge(gate_ready, 4)
            for b in range(B):
                q, e = slice(32 * b, 32 * b + 1), slice(64 + 32 * b, 64 + 32 * b + 1)
                if b:
                    pe.wait_ge(row_ready, b)
                for c in range(DC):
                    last = mm(pb[0][q, :], cond_v[:, c, b:b + 1], WsT[:, DC + c, :], c == 0, c == DC - 1)
                last.then_inc(row_done, 1)
                mm(pb[3][e, :], ones[0:3, 0:1], rows_in[:], True, True).then_inc(row_done, 1)
                for d in range(2):
                    for c in range(DC):
                        last = mm(pb[1 + d][q, 0:HM], cq[:, c, b:b + 1], Gs[:, d, c, b, :], c == 0, c == DC - 1)
                    last.then_inc(row_done, 1)
                    for c in range(DC):
                        mm(pb[4 + d][e, 0:HM], col("b_self", c), Gs[:, d, c, b, :], c == 0, c == DC - 1)
                    for j in range(DC):
                        last = nc.tensor.matmul(pb[4 + d][e, j * GM:(j + 1) * GM], col("bq", d * DC + j), Kblk[:, d, j, b, :],
                                                start=False, stop=True, skip_group_check=True)
                    last.then_inc(row_done, 1)
            pe.wait_ge(row_ready, 2)
            pe.wait_ge(ld_o, 16)
            for n in range(4):
                b, d = n // 2, n % 2
                if n >= 2:
                    pe.wait_ge(vp_ready, n - 1)
                for c in range(DC):
                    last = mm(pb[2 + n % 2][32 * n:32 * n + NONGT, :], sf20[:, c, b * NONGT:(b + 1) * NONGT], WoT[:, d, c, :], c == 0, c == DC - 1)
                last.then_inc(vp_done, 1)
            n = 0
            for b in range(B):
                for d in range(2):
                    for ic in range(DC):
                        if n >= 2:
                            pe.wait_ge(h_lo, n - 1)
                        for c in range(DC):
                            last = mm(pb[n % 2][:, 0:HM], Wsn[:, c, ic * P:(ic + 1) * P], Gs[:, d, c, b, :], c == 0, c == DC - 1)
                        last.then_inc(h_done, 1)
                        n += 1


def graph_phase(nc, io, keep):
    with ExitStack() as ctx:
        m = Mem(nc, ctx, "gat")
        NT = B * S // P
        NB = S // P
        LW, VB, r4, ident = keep["LW"], keep["VB"], keep["r4"], keep["ident"]
        MW = 2 * NONGT * L
        xT = [m.sb(f"xT{i}", [P, DC, P]) for i in range(2)]
        xs = [m.sb(f"xs{i}", [P, 2, DC, P], F32R) for i in range(2)]
        xrow = [m.sb(f"xrow{i}", [P, D]) for i in range(2)]
        msk = [m.sb(f"msk{i}", [P, MW], I32) for i in range(2)]
        mf = [m.sb(f"mf{i}", [P, MW]) for i in range(2)]
        mw = [m.sb(f"mw{i}", [P, MW]) for i in range(2)]
        onesr = m.sb("onesr", [P, P], F32R)
        zeros = m.sb("zeros", [P, 1, 1])
        n4 = [m.sb(f"n4{i}", [4, P], F32R) for i in range(2)]
        count = m.sb("count", [P, 2 * NONGT])
        vb = m.sb("vb", [P, 2 * NONGT])
        neg = m.sb("neg", [P, 2 * NONGT])
        open_ = m.sb("open", [P, 2 * NONGT])
        bias = m.sb("bias", [P, 2 * NONGT])
        aff = m.sb("aff", [P, 2, HM])
        prob = m.sb("prob", [P, 2, HM])
        top = m.sb("top", [P, 2 * H])
        total = m.sb("total", [P, 2 * H])
        wT = m.sb("wT", [GM, 2, DC * P])
        x1 = [m.sb(f"x1{i}", [P, D]) for i in range(2)]
        p_aff = m.ps("p_aff", [P, 2, 512])
        p_sf = [m.ps(f"p_sf{i}") for i in range(2)]
        p_wT = m.ps("p_wT", [P, 2, 512])
        p_n = m.ps("p_n")

        ones_ready = m.sem("ones_ready")
        loaded = m.sems("loaded", 2)
        row_loaded = m.sems("row_loaded", 2)
        stored = m.sems("stored", 2)
        x_split, x_part, mask_ready, mask_part = [m.sem(x) for x in ("x_split", "x_part", "mask_ready", "mask_part")]
        n_done, n_ready, aff_done, aff_read, sub_ready, exp_ready = [
            m.sem(x) for x in ("n_done", "n_ready", "aff_done", "aff_read", "sub_ready", "exp_ready")]
        sf_done, w_ready, wT_done, wT_ready, att_done, x1_ready, mask_read, dv = [
            m.sem(x) for x in ("sf_done", "w_ready", "wT_done", "wT_ready", "att_done", "x1_ready", "mask_read", "dv")]
        block = m.block()
        xT_v = io["xT"].rearrange("b (c p) n -> p c b n", p=P)

        def per_batch(eng, body):
            for b in range(B):
                tiles(eng, NB, 2, lambda t, s: body(t + b * NB, s, b, t))

        @block.sync
        def _(sp):
            def load(t, s, b, tb):
                sp.dma_start(xT[s][:], xT_v[:, :, b, bass.ds(tb * P, P)]).then_inc(loaded[s], 16)
                sp.dma_start(msk[s][:], io["mask"][bass.ds(t * P, P), :]).then_inc(loaded[s], 16)

            def load_row(t, s):
                sp.dma_start(xrow[s][:], io["x"][bass.ds(t * P, P), :]).then_inc(row_loaded[s], 16)

            def store(t, s):
                sp.wait_ge(x1_ready, t + 1)
                sp.dma_start(io["x1_d"][bass.ds(t * P, P), :], x1[s][:]).then_inc(stored[s], 16)

            for t in range(2):
                load(t, t, 0, t)
                load_row(t, t)

            def body(t, s, b, tb):
                sp.wait_ge(x_split, t + 1)
                sp.wait_ge(mask_ready, t + 1)
                if before(tb, NB - 2):
                    load(t + 2, s, b, tb + 2)
                elif b + 1 < B:
                    load(t + 2, s, b + 1, tb + 2 - NB)
                if at_least(t, 1):
                    store(t - 1, 1 - s)
                    if before(t, NT - 1):
                        load_row(t + 1, 1 - s)
            per_batch(sp, body)
            store(NT - 1, 1)
            for s in range(2):
                sp.wait_ge(stored[s], 16 * NT // 2)

        @block.gpsimd
        def _(pool):
            nc.gpsimd.memset(zeros[:], 0.0).then_inc(ones_ready, 1)
            nc.gpsimd.memset(raw(onesr[:]), 1.0).then_inc(ones_ready, 1)
            pool.wait_ge(ones_ready, 2)

            def body(t, s, b, tb):
                pool.wait_ge(loaded[s], (t - s) * 16 + 32)
                if at_least(t, 2):
                    pool.wait_ge(sf_done, t - 1)
                if at_least(t, 2):
                    pool.wait_ge(mask_read, t - 1)
                nc.gpsimd.tensor_tensor(xs[s][:, 0], xT[s][:], zeros[:].to_broadcast([P, DC, P]), ALU.add).then_inc(x_part, 1)
                nc.gpsimd.tensor_copy(mf[s][:], msk[s][:]).then_inc(mask_part, 1)
                pool.wait_ge(x_part, t + 1)
                nc.gpsimd.tensor_tensor(xs[s][:, 1], xT[s][:], xs[s][:, 0], ALU.subtract).then_inc(x_split, 1)
                pool.wait_ge(mask_part, t + 1)
                nc.gpsimd.tensor_tensor(mw[s][:], mf[s][:], keep["wl_bc"][:], ALU.mult).then_inc(mask_ready, 1)
            per_batch(pool, body)

        @block.scalar
        def _(act):
            def body(t, s, b, tb):
                act.wait_ge(sub_ready, t + 1)
                nc.scalar.activation(prob[:], aff[:], ACT.Exp).then_inc(exp_ready, 1)
                act.wait_ge(wT_done, t + 1)
                if at_least(t, 1):
                    act.wait_ge(att_done, t)
                nc.scalar.activation(wT[:], p_wT[0:GM], ACT.Identity).then_inc(wT_ready, 1)
            per_batch(act, body)

        @block.vector
        def _(dve):
            NL = 6

            def mask_terms(t, s, first):
                link = steps(dve, dv, first)
                dve.wait_ge(mask_ready, t + 1)
                nc.vector.tensor_reduce(count[:], mf[s][:].rearrange("p (k l) -> p k l", l=L), AX.X, ALU.add)
                nc.vector.tensor_reduce(vb[:], mw[s][:].rearrange("p (k l) -> p k l", l=L), AX.X, ALU.add).then_inc(mask_read, 1)
                dve.wait_ge(mask_read, t + 1)
                nc.vector.tensor_scalar(open_[:], count[:], 0.0, None, ALU.is_gt)
                link(nc.vector.tensor_scalar(neg[:], count[:], 0.0, NEG, ALU.is_le, ALU.mult))
                link(nc.vector.scalar_tensor_tensor(bias[:], vb[:], keep["bb"][:], neg[:], ALU.add, ALU.add))

            def row_flags(t, s):
                dve.wait_ge(n_done, t + 1)
                nc.vector.tensor_scalar(n4[s][:], p_n[0:4, 0:P], 0.0, keep["floor4"][:], ALU.not_equal, ALU.max).then_inc(n_ready, 1)

            def rest(t, s):
                dve.wait_ge(att_done, t + 1)
                dve.wait_ge(row_loaded[s], (t - s) * 8 + 16)
                if at_least(t, 2):
                    dve.wait_ge(stored[s], (t - s) * 8)
                nc.vector.scalar_tensor_tensor(x1[s][:], p_sf[s][:], 0.0, xrow[s][:], ALU.max, ALU.add).then_inc(x1_ready, 1)

            mask_terms(0, 0, 0)
            row_flags(0, 0)

            def body(t, s, b, tb):
                link = steps(dve, dv, t * NL + 2)

                def heads(ap):
                    return ap.rearrange("p (d m) -> p d m", d=2).unsqueeze(2).to_broadcast([P, 2, H, NONGT])

                def of_head(ap):
                    return ap.rearrange("p (d h) -> p d h", d=2).unsqueeze(3).to_broadcast([P, 2, H, NONGT])

                a4 = aff[:].rearrange("p d (h m) -> p d h m", m=NONGT)
                dve.wait_ge(aff_done, t + 1)
                if at_least(t, 1):
                    dve.wait_ge(exp_ready, t)
                nc.vector.tensor_tensor(a4, p_aff[:, :, 0:HM].rearrange("p d (h m) -> p d h m", m=NONGT),
                                        heads(open_[:]), ALU.mult).then_inc(aff_read, 1)
                dve.wait_ge(aff_read, t + 1)
                link(nc.vector.tensor_tensor(a4, a4, heads(bias[:]), ALU.add))
                link(nc.vector.tensor_reduce(top[:], aff[:].rearrange("p d (h m) -> p (d h) m", m=NONGT), AX.X, ALU.max))
                nc.vector.tensor_tensor(a4, a4, of_head(top[:]), ALU.subtract).then_inc(sub_ready, 1)
                if before(t, NT - 1):
                    mask_terms(t + 1, 1 - s, t * NL + 4)
                link = steps(dve, dv, t * NL + (6 if before(t, NT - 1) else 4))
                p4 = prob[:].rearrange("p d (h m) -> p d h m", m=NONGT)
                dve.wait_ge(exp_ready, t + 1)
                link(nc.vector.tensor_reduce(total[:], prob[:].rearrange("p d (h m) -> p (d h) m", m=NONGT), AX.X, ALU.add))
                link(nc.vector.reciprocal(total[:], total[:]))
                nc.vector.tensor_tensor(p4, p4, of_head(total[:]), ALU.mult).then_inc(w_ready, 1)
                if at_least(t, 1):
                    rest(t - 1, 1 - s)
                if before(t, NT - 1):
                    row_flags(t + 1, 1 - s)
            per_batch(dve, body)
            rest(NT - 1, 1)

        @block.tensor
        def _(pe):
            pe.wait_ge(ones_ready, 2)

            def row_sums(t, s):
                pe.wait_ge(x_split, t + 1)
                if at_least(t, 1):
                    pe.wait_ge(n_ready, t)
                for k in range(2):
                    for c in range(DC):
                        last = nc.tensor.matmul(p_n[:, 0:P], onesr[:], xs[s][:, k, c, :], start=k + c == 0, stop=k + c == DC)
                last.then_inc(n_done, 1)

            def scores(t, s, b):
                if at_least(t, 1):
                    pe.wait_ge(aff_read, t)
                outs = [(p_aff[:, d, 0:HM], slice(D + d * HM, D + (d + 1) * HM)) for d in range(2)]
                for k, w in PASSES:
                    for c in range(DC):
                        for o, at in outs:
                            nc.tensor.matmul(o, xs[s][:, k, c, :], LW[:, w, b, c, at], start=(k + w + c == 0), stop=False)
                pe.wait_ge(n_ready, t + 1)
                for o, at in outs:
                    last = nc.tensor.matmul(o, n4[s][:], r4[:, b, at], start=False, stop=True)
                last.then_inc(aff_done, 1)

            def self_features(t, s, b):
                if at_least(t, 2):
                    pe.wait_ge(x1_ready, t - 1)
                for k, w in PASSES:
                    for c in range(DC):
                        nc.tensor.matmul(p_sf[s][:], xs[s][:, k, c, :], LW[:, w, b, c, 0:D], start=(k + w + c == 0), stop=False)
                nc.tensor.matmul(p_sf[s][:], n4[s][:], r4[:, b, 0:D], start=False, stop=True).then_inc(sf_done, 1)

            row_sums(0, 0)
            scores(0, 0, 0)
            self_features(0, 0, 0)
            row_sums(1, 1)

            def body(t, s, b, tb):
                more = before(tb, NB - 1) or b + 1 < B
                following = (t + 1, 1 - s, b if before(tb, NB - 1) else b + 1)
                if more:
                    scores(*following)
                pe.wait_ge(w_ready, t + 1)
                if at_least(t, 1):
                    pe.wait_ge(wT_ready, t)
                for d in range(2):
                    for j in range(DC):
                        last = nc.tensor.transpose(p_wT[0:GM, d, j * P:(j + 1) * P], prob[:, d, j * GM:(j + 1) * GM], ident[:])
                last.then_inc(wT_done, 1)
                if more:
                    self_features(*following)
                pe.wait_ge(wT_ready, t + 1)
                for d in range(2):
                    for j in range(DC):
                        last = nc.tensor.matmul(p_sf[s][:, j * P:(j + 1) * P], wT[:, d, j * P:(j + 1) * P], VB[:, b, d, j, :],
                                                start=False, stop=True, skip_group_check=True)
                last.then_inc(att_done, 1)
                if before(t, NT - 2):
                    row_sums(t + 2, s)
            per_batch(pe, body)


def norm_rows(nc, dve, link, x, stats, mv, rstd, tmp, var_ready, root_ready, n):
    ve, r = tmp[:, 0:4], rstd[:]
    for nt in range(3):
        last = nc.vector.bn_stats(stats[:, nt, :], x[:, nt, :])
    link(last)
    nc.vector.bn_stats(stats[:, 3, :], x[:, 3, :])
    for nt in range(3):
        last = nc.vector.bn_aggr(mv[:, nt, :], stats[:, nt, :])
    link(last)
    nc.vector.tensor_scalar_add(ve[:, 0:3], mv[:, 0:3, 1], EPS)
    link(nc.vector.bn_aggr(mv[:, 3, :], stats[:, 3, :]))
    nc.vector.tensor_scalar_add(ve[:, 3:4], mv[:, 3:4, 1], EPS).then_inc(var_ready, 1)
    dve.wait_ge(root_ready, n + 1)
    link(nc.vector.reciprocal(r, tmp[:, 4:8]))
    link(nc.vector.tensor_tensor(tmp[:, 8:12], r, r, ALU.mult))
    link(nc.vector.tensor_tensor(tmp[:, 8:12], tmp[:, 8:12], ve, ALU.mult))
    link(nc.vector.tensor_scalar(tmp[:, 8:12], tmp[:, 8:12], -0.5, 1.5, ALU.mult, ALU.add))
    link(nc.vector.tensor_tensor(r, r, tmp[:, 8:12], ALU.mult))


NORM_LINKS = 8


def qkv_phase(nc, io, keep):
    with ExitStack() as ctx:
        m = Mem(nc, ctx, "qkv")
        NCH = B * S // 512
        cols, ident, modA, modB = keep["cols"], keep["ident"], keep["modA"], keep["modB"]
        stage = m.sb("stage", [P, DC, 3 * D])
        W = m.sb("W", [P, 2, DC, 3 * D], F32R)
        bv = m.sb("bv", [P, D])
        xr = [m.sb(f"xr{i}", [P, 4, D]) for i in range(2)]
        xn = m.sb("xn", [P, 4, D])
        th = [m.sb(f"th{i}", [P, 512]) for i in range(2)]
        hs = [m.sb(f"hs{i}", [P, 2, DC, 512], F32R) for i in range(2)]
        tq = [m.sb(f"tq{i}", [P, 512]) for i in range(2)]
        qs = [m.sb(f"qs{i}", [P, 2, 512], F32R) for i in range(4)]
        vs = [m.sb(f"vs{i}", [P, 512]) for i in range(2)]
        stats, mv = m.sb("stats", [P, 4, 6]), m.sb("mv", [P, 4, 2])
        rstd, tmp = m.sb("rstd", [P, 4]), m.sb("tmp", [P, 12])
        pT = [m.ps(f"pT{i}") for i in range(2)]
        pq = [m.ps(f"pq{i}") for i in range(4)]
        pv = [m.ps(f"pv{i}") for i in range(2)]

        w_loaded = m.sems("w_loaded", DC)
        b_loaded, w_hi, w_lo = [m.sem(x) for x in ("b_loaded", "w_hi", "w_lo")]
        x_loaded, q_stored, v_stored = m.sems("x_loaded", 2), m.sems("q_stored", 4), m.sems("v_stored", 2)
        var_ready, root_ready, xn_ready, tr_done, h_hi, h_lo = [
            m.sem(x) for x in ("var_ready", "root_ready", "xn_ready", "tr_done", "h_hi", "h_lo")]
        q_done, q_hi, q_lo, v_done, v_ready, dv, ac = [
            m.sem(x) for x in ("q_done", "q_hi", "q_lo", "v_done", "v_ready", "dv", "ac")]
        block = m.block()
        ORDER = [("q", 0), ("q", 1), ("h", 0), ("q", 2), ("h", 1), ("q", 3), ("h", 2), ("q", 4), ("h", 3),
                 ("q", 5), ("q", 6), ("q", 7), ("v", 0), ("v", 1), ("v", 2), ("v", 3)]
        x_v = io["x1_d"].rearrange("(n p) d -> p n d", p=P)

        @block.sync
        def _(sp):
            def load(i, s):
                sp.dma_start(xr[s][:], x_v[:, bass.ds(i * 4, 4), :]).then_inc(x_loaded[s], 16)

            load(0, 0)
            for c in range(DC):
                sp.dma_start(stage[:, c, :], io["Wqkv"][c * P:(c + 1) * P, :]).then_inc(w_loaded[c], 16)
            sp.dma_start(bv[:], io["rows"][5:6, :].to_broadcast([P, D])).then_inc(b_loaded, 16)
            load(1, 1)

            def body(i, s):
                if before(i, NCH - 2):
                    sp.wait_ge(xn_ready, i + 1)
                    load(i + 2, s)
                for kind, j in ORDER:
                    if kind == "q":
                        sp.wait_ge(q_lo, i * 8 + j + 1)
                        dst = io["qk_d"][j // 4, :, (j % 4) * P:(j % 4 + 1) * P, bass.ds(i * 512, 512)]
                        sp.dma_start(dst.rearrange("a p n -> p a n"), raw(qs[j % 4][:])).then_inc(q_stored[j % 4], 16)
                    elif kind == "v":
                        sp.wait_ge(v_ready, i * 4 + j + 1)
                        sp.dma_start(io["v_d"][bass.ds(i * 512 + j * P, P), :], vs[j % 2][:]).then_inc(v_stored[j % 2], 16)
            tiles(sp, NCH, 2, body)
            for x in q_stored:
                sp.wait_ge(x, 16 * 2 * NCH)
            for x in v_stored:
                sp.wait_ge(x, 16 * 2 * NCH)

        @block.scalar
        def _(act):
            for c in range(DC):
                act.wait_ge(w_loaded[c], 16)
                nc.scalar.activation(W[:, 0, c, :], stage[:, c, :], ACT.Identity).then_inc(w_hi, 1)

            def root(i):
                act.wait_ge(var_ready, i + 1)
                nc.scalar.activation(tmp[:, 4:8], tmp[:, 0:4], ACT.Sqrt).then_inc(root_ready, 1)

            def h_parts(i, s, c):
                act.wait_ge(tr_done, i * 4 + c + 1)
                if c >= 2 or at_least(i, 1):
                    act.wait_ge(h_lo, i * 4 + c - 1)
                if c == 0 and at_least(i, 2):
                    act.wait_ge(v_done, i * 4 - 4)
                a, b = modA[:, 0, bass.ds(i * DC + c, 1)], modB[:, 0, bass.ds(i * DC + c, 1)]
                nc.scalar.activation(th[c % 2][:], pT[c % 2][:], ACT.Identity, bias=b, scale=a)
                nc.scalar.activation(hs[s][:, 0, c, :], pT[c % 2][:], ACT.Identity, bias=b, scale=a).then_inc(h_hi, 1)

            root(0)
            for c in range(DC):
                h_parts(0, 0, c)

            def body(i, s):
                if before(i, NCH - 1):
                    root(i + 1)
                for kind, j in ORDER:
                    if kind == "q":
                        n = i * 8 + j
                        act.wait_ge(q_done, n + 1)
                        if j >= 2 or at_least(i, 1):
                            act.wait_ge(q_lo, n - 1)
                        if j >= 4 or at_least(i, 1):
                            act.wait_ge(q_stored[j % 4], (i * 2 + j // 4) * 16)
                        bias = cols[:, COLS["bqk"][0] + j:COLS["bqk"][0] + j + 1]
                        nc.scalar.activation(tq[j % 2][:], pq[j % 4][:], ACT.Identity, bias=bias)
                        nc.scalar.activation(qs[j % 4][:, 0, :], pq[j % 4][:], ACT.Identity, bias=bias).then_inc(q_hi, 1)
                    elif kind == "h" and before(i, NCH - 1):
                        h_parts(i + 1, 1 - s, j)
            tiles(act, NCH, 2, body)

        @block.gpsimd
        def _(pool):
            for c in range(DC):
                pool.wait_ge(w_hi, c + 1)
                nc.gpsimd.tensor_tensor(W[:, 1, c, :], stage[:, c, :], W[:, 0, c, :], ALU.subtract).then_inc(w_lo, 1)

        @block.vector
        def _(dve):
            def norm(i, s):
                link = steps(dve, dv, i * NORM_LINKS)
                dve.wait_ge(x_loaded[s], (i - s) * 8 + 16)
                norm_rows(nc, dve, link, xr[s], stats, mv, rstd, tmp, var_ready, root_ready, i)
                if at_least(i, 1):
                    dve.wait_ge(tr_done, i * 4)
                for nt in range(4):
                    last = nc.vector.tensor_scalar(xn[:, nt, :], xr[s][:, nt, :], mv[:, nt, 0:1], rstd[:, nt:nt + 1],
                                                   ALU.subtract, ALU.mult)
                last.then_inc(xn_ready, 1)

            def h_low(i, s, c):
                dve.wait_ge(h_hi, i * 4 + c + 1)
                nc.vector.tensor_tensor(hs[s][:, 1, c, :], th[c % 2][:], hs[s][:, 0, c, :], ALU.subtract).then_inc(h_lo, 1)

            norm(0, 0)
            for c in range(DC):
                h_low(0, 0, c)
            dve.wait_ge(b_loaded, 16)

            def body(i, s):
                if before(i, NCH - 1):
                    norm(i + 1, 1 - s)
                for kind, j in ORDER:
                    if kind == "q":
                        dve.wait_ge(q_hi, i * 8 + j + 1)
                        nc.vector.tensor_tensor(qs[j % 4][:, 1, :], tq[j % 2][:], qs[j % 4][:, 0, :], ALU.subtract).then_inc(q_lo, 1)
                    elif kind == "h":
                        if before(i, NCH - 1):
                            h_low(i + 1, 1 - s, j)
                    else:
                        dve.wait_ge(v_done, i * 4 + j + 1)
                        if j >= 2 or at_least(i, 1):
                            dve.wait_ge(v_stored[j % 2], (i * 2 + j // 2) * 16)
                        nc.vector.tensor_tensor(vs[j % 2][:], pv[j % 2][:], bv[:], ALU.add).then_inc(v_ready, 1)
            tiles(dve, NCH, 2, body)

        @block.tensor
        def _(pe):
            def transposes(i, c):
                if c == 0:
                    pe.wait_ge(xn_ready, i + 1)
                if c >= 2 or at_least(i, 1):
                    pe.wait_ge(h_hi, i * 4 + c - 1)
                for nt in range(4):
                    last = nc.tensor.transpose(pT[c % 2][:, nt * P:(nt + 1) * P], xn[:, nt, c * P:(c + 1) * P], ident[:])
                last.then_inc(tr_done, 1)

            for c in range(DC):
                transposes(0, c)
            pe.wait_ge(w_lo, DC)

            def body(i, s):
                pe.wait_ge(h_lo, i * 4 + 4)
                for kind, j in ORDER:
                    if kind == "h":
                        if before(i, NCH - 1):
                            transposes(i + 1, j)
                        continue
                    if kind == "q":
                        if j >= 4 or at_least(i, 1):
                            pe.wait_ge(q_hi, i * 8 + j - 3)
                        out, done = pq[j % 4], q_done
                    else:
                        if j >= 2 or at_least(i, 1):
                            pe.wait_ge(v_ready, i * 4 + j - 1)
                        out, done = pv[j % 2], v_done
                    for n, (k, w) in enumerate(PASSES):
                        for c in range(DC):
                            if kind == "q":
                                a, r = W[:, k, c, j * P:(j + 1) * P], hs[s][:, w, c, :]
                            else:
                                a, r = hs[s][:, k, c, j * P:(j + 1) * P], W[:, w, c, 2 * D:3 * D]
                            last = nc.tensor.matmul(out[:], a, r, start=n + c == 0, stop=n == 2 and c == DC - 1)
                    last.then_inc(done, 1)
            tiles(pe, NCH, 2, body)


def attention_phase(nc, io, keep):
    with ExitStack() as ctx:
        m = Mem(nc, ctx, "att")
        NG = B * H // 2
        MT = S // P
        ST = 2 * MT
        KD = 3 * HD
        NM = 2 * MT * 4
        MS = NM // ST
        LEAD = 6
        EARLY = MS
        U = 4
        PR = 4
        ADDED = [0, 1, 2, 4, 5, 6, 8, 9, 11, 12, 13]
        NA = len(ADDED) - 1
        FINISH = 2
        INVERT = 4
        STORE = 10
        SUMMED = [t for t in range(MT) if t not in ADDED]
        ident = keep["ident"]
        qs = [m.sb(f"qs{i}", [KD + 2, 2, S], F32R) for i in range(U)]
        ks = [m.sb(f"ks{i}", [KD + 2, 2, S], F32R) for i in range(U)]
        V = [m.sb(f"V{i}", [P, MT, 2 * HD]) for i in range(2)]
        ones = m.sb("ones", [P, HD])
        prob = [m.sb(f"prob{i}", [P, 4, 512]) for i in range(PR)]
        acc = [m.sb(f"acc{i}", [P, 4, 512]) for i in range(2)]
        mx = m.sb("mx", [P, 32, 4])
        top = m.sb("top", [P, 32])
        nm = m.sb("nm", [32, 2, P], F32R)
        rec, oc = m.sb("rec", [P, 512]), m.sb("oc", [P, 512])
        o = [m.sb(f"o{i}", [P, 512]) for i in range(2)]
        zero = m.sb("zero", [P, 1])
        pS = [m.ps(f"pS{i}") for i in range(3)]
        pM = [m.ps(f"pM{i}") for i in range(3)]
        pO, pZ = m.ps("pO"), m.ps("pZ")

        loaded, v_loaded, o_stored = m.sems("loaded", U), m.sems("v_loaded", 2), m.sems("o_stored", 2)
        cleared, s_done, exp_done, m_done, m_read = [m.sem(x) for x in ("cleared", "s_done", "exp_done", "m_done", "m_read")]
        top_ready, nm_hi, step_done, added, o_done, o_copied = [
            m.sem(x) for x in ("top_ready", "nm_hi", "step_done", "added", "o_done", "o_copied")]
        z_done, z_read, inverted, o_ready = [m.sem(x) for x in ("z_done", "z_read", "inverted", "o_ready")]
        top_rows = m.sems("top_rows", U)
        block = m.block()
        q_v = io["qk_d"][0].rearrange("a (g h p) n -> a g p h n", h=2, p=HD)
        k_v = io["qk_d"][1].rearrange("a (g h p) n -> a g p h n", h=2, p=HD)
        v_v = io["v_d"].rearrange("(b t p) d -> p b t d", b=B, p=P)
        o_v = io["o_d"].rearrange("(g h p) (b n) -> g h p b n", h=2, p=HD, b=B)

        def m_unit(g, step, c):
            ahead = 1 if step < ST - LEAD else 2
            return (g + ahead, (step + LEAD) % ST * MS + c) if before(g, NG - ahead) else None

        def turn(g):
            return g * (NM + 1) + NM + (EARLY if before(g, NG - 1) else 0)

        def tile(g, n):
            return g * (NM + 1) + n - (1 if n < EARLY and at_least(g, 1) else 0)

        def bank(g, n):
            return pM[(n - (1 if n < EARLY and at_least(g, 1) else 0)) % 3]

        def turned(g):
            return pM[(NM + (EARLY if before(g, NG - 1) else 0)) % 3]
        assert (NM + 1) % 3 == 0

        def groups(eng, body):
            for g in range(U):
                body(g, g, lambda j: (g + j) // 2)
            with eng.Fori(1, NG // U - 1) as i:
                for k in range(U):
                    body(i * U + k, k, lambda j: i * (U // 2) + (k + j) // 2)
            for g in range(NG - U, NG):
                body(g, g % U, lambda j: (g + j) // 2)

        def half_before(g, step):
            return 2 * g + step // MT - 1

        @block.sync
        def _(sp):
            def load(k, hp):
                at = slice(k % 2 * S, (k % 2 + 1) * S)
                for i, part in enumerate((0, 0, 1)):
                    sp.dma_start(raw(qs[k][i * HD:(i + 1) * HD]), q_v[part, bass.ds(hp, 1), :, :, at]
                                 .rearrange("a p h n -> (a p) h n")).then_inc(loaded[k], 16)
                for i, part in enumerate((0, 1, 0)):
                    sp.dma_start(raw(ks[k][i * HD:(i + 1) * HD]), k_v[part, bass.ds(hp, 1), :, :, at]
                                 .rearrange("a p h n -> (a p) h n")).then_inc(loaded[k], 16)

            def load_v(k, hp):
                sp.dma_start(V[k][:], v_v[:, k, :, bass.ds(hp * 2 * HD, 2 * HD)]).then_inc(v_loaded[k], 16)

            def rows(g, k):
                sp.wait_ge(m_read, turn(g) + 1)
                for h in range(2):
                    sp.dma_start(raw(qs[k][KD + h:KD + h + 1]).rearrange("a h (t n) -> a (h t) n", n=P),
                                 raw(nm[:, h, :])).then_inc(top_rows[k], 16)

            load(0, 0)
            load(1, 0)
            load_v(0, 0)
            load_v(1, 0)
            load(2, 1)
            load(3, 1)
            rows(0, 0)

            def body(g, k, pair):
                if at_least(g, 1):
                    sp.wait_ge(step_done, g * ST)
                    if before(g, NG - U + 1):
                        load((k - 1) % U, pair(U - 1))
                    if before(g, NG - 1):
                        load_v((k + 1) % 2, pair(1))
                if before(g, NG - 1):
                    rows(g + 1, (k + 1) % U)
            groups(sp, body)

        @block.gpsimd
        def _(pool):
            nc.gpsimd.memset(ones[:], 1.0).then_inc(cleared, 1)
            nc.gpsimd.memset(zero[:], 0.0).then_inc(cleared, 1)
            for k in range(U):
                pool.wait_ge(cleared, 2 + k)
                nc.gpsimd.memset(raw(ks[k][KD:KD + 2]), 1.0).then_inc(cleared, 1)
            pool.wait_ge(cleared, 2 + U)

            def body(g, k, pair):
                for half in range(2):
                    for i in range(1, NA + 1):
                        step = half * MT + ADDED[i]
                        n = (g * 2 + half) * NA
                        pool.wait_ge(exp_done, (g * ST + step) * 4 + 4)
                        new = prob[step % PR]
                        if i == 1:
                            if at_least(g, 1):
                                pool.wait_ge(z_done, g * 2 + half - 1)
                            old = prob[(half * MT + ADDED[0]) % PR]
                        else:
                            pool.wait_ge(added, n + i - 1)
                            old = acc[half]
                        nc.gpsimd.tensor_tensor(acc[half][:], old[:], new[:], ALU.add).then_inc(added, 1)
            groups(pool, body)

        @block.scalar
        def _(act):
            def free(g, step):
                if step < PR and not at_least(g, 1):
                    return
                act.wait_ge(step_done, g * ST + step - PR + 1)
                half, t = divmod((step - PR) % ST, MT)
                if t in ADDED:
                    whole = (g if step >= PR else g - 1) * 2 + half
                    act.wait_ge(added, whole * NA + max(1, ADDED.index(t)))

            def body(g, k, pair):
                for step in range(ST):
                    free(g, step)
                    for c in range(4):
                        n = 4 * step + c
                        act.wait_ge(s_done, g * 4 * ST + n + 1)
                        nc.scalar.activation(prob[step % PR][:, c, :], pS[n % 3][:], ACT.Exp, scale=SCALE).then_inc(exp_done, 1)
                        if step % MT == 0 and c == 2 and (step or at_least(g, 1)):
                            copy(half_before(g, step))
                    if step % MT == FINISH + 1 and (step >= MT or at_least(g, 1)):
                        copy_sums(half_before(g, step))
                    if step == STORE and at_least(g, 1):
                        store(2 * g - 1, (k - 1) % U, pair(-1), 1)
                    if step == MT + STORE:
                        store(2 * g, k, pair(0), 0)

            def copy(n):
                act.wait_ge(o_done, n + 1)
                if at_least(n, 1):
                    act.wait_ge(o_ready, n)
                nc.scalar.activation(oc[:], pO[:], ACT.Identity).then_inc(o_copied, 1)

            def store(n, k, hp, half):
                act.wait_ge(o_ready, n + 1)
                for c in range(4):
                    dst = o_v[bass.ds(hp, 1), c // 2, :, k % 2, (2 * half + c % 2) * 512:(2 * half + c % 2 + 1) * 512]
                    act.dma_start(dst.rearrange("g p n -> (g p) n"), o[half][c * HD:(c + 1) * HD]).then_inc(o_stored[half], 16)

            def copy_sums(n):
                act.wait_ge(z_done, n + 1)
                if at_least(n, 1):
                    act.wait_ge(o_ready, n)
                nc.scalar.activation(rec[:], pZ[:], ACT.Identity).then_inc(z_read, 1)
            groups(act, body)
            copy(2 * NG - 1)
            copy_sums(2 * NG - 1)
            store(2 * NG - 1, U - 1, (NG - 1) // 2, 1)
            for x in o_stored:
                act.wait_ge(x, 16 * 4 * NG)

        @block.vector
        def _(dve):
            def maxima(g, n):
                if n == 0 and at_least(g, 1):
                    dve.wait_ge(top_ready, g)
                dve.wait_ge(m_done, tile(g, n) + 1)
                nc.vector.tensor_reduce(mx[:, n // 4, n % 4:n % 4 + 1], bank(g, n)[:], AX.X, ALU.max).then_inc(m_read, 1)

            def top_of(g):
                dve.wait_ge(m_read, tile(g, NM - 1) + 1)
                nc.vector.tensor_reduce(top[:], mx[:], AX.X, ALU.max, negate=True).then_inc(top_ready, 1)

            def parts(g, k):
                dve.wait_ge(m_done, turn(g) + 1)
                if at_least(g, 1):
                    dve.wait_ge(top_rows[(k - 1) % U], (g - 1 - (k - 1) % U) * 8 + 32)
                nc.vector.tensor_copy(nm[:, 0, :], turned(g)[0:32, 0:P]).then_inc(nm_hi, 1)
                dve.wait_ge(nm_hi, g + 1)
                nc.vector.tensor_tensor(nm[:, 1, :], turned(g)[0:32, 0:P], nm[:, 0, :], ALU.subtract).then_inc(m_read, 1)

            def invert(n, half, group, c):
                if c == 4:
                    return output(n, half, group)
                at = slice(c * P, (c + 1) * P)
                if c == 0:
                    dve.wait_ge(z_read, n + 1)
                nc.vector.reciprocal(rec[:, at], rec[:, at]).then_inc(inverted, 1)

            def output(n, half, group):
                dve.wait_ge(o_copied, n + 1)
                if at_least(group, 1):
                    dve.wait_ge(o_stored[half], group * 64)
                dve.wait_ge(inverted, (n + 1) * 4)
                nc.vector.tensor_tensor(o[half][:], oc[:], rec[:], ALU.mult).then_inc(o_ready, 1)

            for n in range(NM):
                maxima(0, n)
            top_of(0)
            for n in range(EARLY):
                maxima(1, n)
            parts(0, 0)
            for n in range(EARLY, LEAD * MS):
                maxima(1, n)

            def body(g, k, pair):
                for step in range(ST):
                    if step == ST - LEAD and before(g, NG - 1):
                        top_of(g + 1)
                    if step == ST - LEAD + 1 and before(g, NG - 1):
                        parts(g + 1, (k + 1) % U)
                    for c in range(4):
                        unit = m_unit(g, step, c)
                        if unit:
                            maxima(*unit)
                        if c == 2 and 0 <= step % MT - INVERT <= 4 and (step >= MT or at_least(g, 1)):
                            invert(half_before(g, step), 1 - step // MT, g if step >= MT else g - 1, step % MT - INVERT)
            groups(dve, body)
            for c in range(5):
                invert(2 * NG - 1, 1, NG - 1, c)

        @block.tensor
        def _(pe):
            def maxima(g, k, n):
                if n == 0:
                    pe.wait_ge(loaded[k], (g - k) * 24 + 96)
                if n >= 3 or at_least(g, 1):
                    pe.wait_ge(m_read, tile(g, n) - 2)
                h, t, mc = n // 64, n // 4 % MT, n % 4
                nc.tensor.matmul(bank(g, n)[:], qs[k][0:KD, h, t * P:(t + 1) * P], ks[k][0:KD, h, mc * 512:(mc + 1) * 512],
                                 start=True, stop=True).then_inc(m_done, 1)

            def top_of(g):
                pe.wait_ge(top_ready, g + 1)
                pe.wait_ge(m_read, turn(g) - 2)
                nc.tensor.transpose(turned(g)[0:32, 0:P], top[:], ident[:]).then_inc(m_done, 1)

            def values(g, k, step):
                half, mt = divmod(step, MT)
                pe.wait_ge(exp_done, (g * ST + step) * 4 + 4)
                if mt == 0 and (half or at_least(g, 1)):
                    pe.wait_ge(o_copied, g * 2 + half)
                for c in range(4):
                    last = nc.tensor.matmul(pO[c * HD:(c + 1) * HD, :], V[k % 2][:, mt, (c // 2) * HD:(c // 2 + 1) * HD],
                                            prob[step % PR][:, c, :], start=mt == 0, stop=mt == MT - 1, skip_group_check=True)
                return last

            def sums(src, first, last_one):
                for c in range(4):
                    last = nc.tensor.matmul(pZ[c * HD:(c + 1) * HD, :], ones[:], src[:, c, :],
                                            start=first, stop=last_one, skip_group_check=True)
                return last

            def finish(g, step):
                n = half_before(g, step)
                pe.wait_ge(added, (n + 1) * NA)
                sums(acc[(step // MT - 1) % 2], False, True).then_inc(z_done, 1)

            for n in range(NM):
                maxima(0, 0, n)
            for n in range(EARLY):
                maxima(1, 1, n)
            top_of(0)
            for n in range(EARLY, LEAD * MS):
                maxima(1, 1, n)
            pe.wait_ge(cleared, 2 + U)

            def body(g, k, pair):
                def scores(step, c):
                    half, mt = divmod(step, MT)
                    n = 4 * step + c
                    h, lc = c // 2, 2 * half + c % 2
                    if n >= 3 or at_least(g, 1):
                        pe.wait_ge(exp_done, g * 4 * ST + (n - 2 if n >= 3 else (-1, 0, -2)[n]))
                    nc.tensor.matmul(pS[n % 3][:], ks[k][:, h, mt * P:(mt + 1) * P], qs[k][:, h, lc * 512:(lc + 1) * 512],
                                     start=True, stop=True).then_inc(s_done, 1)
                    unit = m_unit(g, step, c)
                    if unit:
                        maxima(unit[0], (k + 1 + (step >= ST - LEAD)) % U, unit[1])

                pe.wait_ge(top_rows[k], (g - k) * 8 + 32)
                pe.wait_ge(v_loaded[k % 2], (g - k % 2) * 8 + 16)
                for step in range(ST):
                    if step == ST - LEAD + 1 and before(g, NG - 1):
                        top_of(g + 1)
                    for c in range(3):
                        scores(step, c)
                    if step or at_least(g, 1):
                        behind(g if step else g - 1, k if step else (k - 1) % U, (step - 1) % ST)
                    scores(step, 3)
                    if step % MT == FINISH and (step >= MT or at_least(g, 1)):
                        finish(g, step)

            def behind(g, k, step):
                last = values(g, k, step)
                t = step % MT
                if t in SUMMED:
                    if t == MT - 1:
                        last.then_inc(o_done, 1)
                    if t == SUMMED[0] and (step > MT or at_least(g, 1)):
                        pe.wait_ge(z_read, g * 2 + step // MT)
                    last = sums(prob[step % PR], t == SUMMED[0], False)
                last.then_inc(step_done, 1)
            groups(pe, body)
            behind(NG - 1, U - 1, ST - 1)
            finish(NG, 0)


def proj_phase(nc, io, keep):
    with ExitStack() as ctx:
        m = Mem(nc, ctx, "prj")
        NCH = B * S // 512
        ident, modA, modB = keep["ident"], keep["modA"], keep["modB"]
        stage = m.sb("stage", [P, DC, D])
        W = m.sb("W", [P, 2, DC, D], F32R)
        bp = m.sb("bp", [P, D])
        gb = m.sb("gb", [P, D])
        gate = [m.sb(f"gate{i}", [P, D]) for i in range(2)]
        os_ = [m.sb(f"os{i}", [P, 2, DC, 512], F32R) for i in range(2)]
        xr = [m.sb(f"xr{i}", [P, 4, D]) for i in range(2)]
        x2 = [m.sb(f"x2{i}", [P, 4, D]) for i in range(2)]
        xn = m.sb("xn", [P, 4, D])
        of = [m.sb(f"of{i}", [P, DC, 512]) for i in range(2)]
        ht = [m.sb(f"ht{i}", [P, 512]) for i in range(4)]
        stats, mv = m.sb("stats", [P, 4, 6]), m.sb("mv", [P, 4, 2])
        rstd, tmp = m.sb("rstd", [P, 4]), m.sb("tmp", [P, 12])
        pT = [m.ps(f"pT{i}") for i in range(4)]
        pp = [m.ps(f"pp{i}") for i in range(4)]

        w_loaded, b_loaded, w_hi, w_lo = [m.sem(x) for x in ("w_loaded", "b_loaded", "w_hi", "w_lo")]
        o_loaded, x_loaded, g_loaded = m.sems("o_loaded", 2), m.sems("x_loaded", 2), m.sems("g_loaded", 2)
        x_stored, h_stored = m.sems("x_stored", 2), m.sems("h_stored", 4)
        var_ready, root_ready, xn_ready, tr_done, h_ready, o_hi, o_lo = [
            m.sem(x) for x in ("var_ready", "root_ready", "xn_ready", "tr_done", "h_ready", "o_hi", "o_lo")]
        p_done, p_read, x2_ready, dv, gb_ready, xb_ready = [
            m.sem(x) for x in ("p_done", "p_read", "x2_ready", "dv", "gb_ready", "xb_ready")]
        block = m.block()

        @block.sync
        def _(sp):
            def load(i, s):
                at = bass.ds(i * 512, 512)
                sp.dma_start(of[s][:], io["o_d"][:, at].rearrange("(c p) n -> p c n", p=P)).then_inc(o_loaded[s], 16)
                sp.dma_start(xr[s][:], io["x1_d"][at, :].rearrange("(n p) d -> p n d", p=P)).then_inc(x_loaded[s], 16)
                sp.dma_start(gate[s][:], io["gate_d"][0, bass.ds(i, 1)].rearrange("a p d -> (a p) d")).then_inc(g_loaded[s], 16)

            sp.dma_start(stage[:], io["Wproj"].rearrange("(c p) n -> p c n", p=P)).then_inc(w_loaded, 16)
            load(0, 0)
            sp.dma_start(bp[:], io["rows"][6:7, :].to_broadcast([P, D])).then_inc(b_loaded, 16)
            load(1, 1)

            def body(i, s):
                sp.wait_ge(x2_ready, i * 4 + 4)
                sp.dma_start(io["x2_d"][bass.ds(i * 512, 512), :].rearrange("(n p) d -> p n d", p=P), x2[s][:]).then_inc(x_stored[s], 16)
                if before(i, NCH - 2):
                    load(i + 2, s)
            tiles(sp, NCH, 2, body)
            for x in x_stored:
                sp.wait_ge(x, 16 * NCH // 2)
            for x in h_stored:
                sp.wait_ge(x, 16 * NCH)

        @block.scalar
        def _(act):
            act.wait_ge(w_loaded, 16)
            nc.scalar.activation(W[:, 0], stage[:], ACT.Identity).then_inc(w_hi, 1)

            def store(i, c):
                act.wait_ge(h_ready, i * 4 + c + 1)
                act.dma_start(io["h2_d"][c * P:(c + 1) * P, bass.ds(i * 512, 512)], ht[c][:]).then_inc(h_stored[c], 16)

            def high(i, s):
                act.wait_ge(o_loaded[s], (i - s) * 8 + 16)
                if at_least(i, 2):
                    act.wait_ge(p_done, i * 4 - 4)
                nc.scalar.activation(os_[s][:, 0], of[s][:], ACT.Identity).then_inc(o_hi, 1)

            high(0, 0)

            def root(i):
                act.wait_ge(var_ready, i + 1)
                nc.scalar.activation(tmp[:, 4:8], tmp[:, 0:4], ACT.Sqrt).then_inc(root_ready, 1)

            high(1, 1)
            root(0)

            def body(i, s):
                for c in range(DC):
                    if c == 2 and before(i, NCH - 1):
                        root(i + 1)
                    if c == 0 and before(i, NCH - 2):
                        high(i + 2, s)
                    if c >= 2:
                        store(i, c - 2)
                    elif at_least(i, 1):
                        store(i - 1, c + 2)
                    act.wait_ge(tr_done, i * 4 + c + 1)
                    if at_least(i, 1):
                        act.wait_ge(h_stored[c], i * 16)
                    a, b = modA[:, 1, bass.ds(i * DC + c, 1)], modB[:, 1, bass.ds(i * DC + c, 1)]
                    nc.scalar.activation(ht[c][:], pT[c][:], ACT.Identity, bias=b, scale=a).then_inc(h_ready, 1)
            tiles(act, NCH, 2, body)
            for c in (2, 3):
                store(NCH - 1, c)

        @block.gpsimd
        def _(pool):
            def with_bias(i, s):
                pool.wait_ge(g_loaded[s], (i - s) * 8 + 16)
                if at_least(i, 1):
                    pool.wait_ge(xb_ready, i)
                nc.gpsimd.tensor_tensor(gb[:], gate[s][:], bp[:], ALU.mult).then_inc(gb_ready, 1)
                pool.wait_ge(x_loaded[s], (i - s) * 8 + 16)
                pool.wait_ge(gb_ready, i + 1)
                nc.gpsimd.tensor_tensor(xr[s][:], xr[s][:], gb[:].unsqueeze(1).to_broadcast([P, 4, D]), ALU.add).then_inc(xb_ready, 1)

            def low(i, s):
                pool.wait_ge(o_hi, i + 1)
                nc.gpsimd.tensor_tensor(os_[s][:, 1], of[s][:], os_[s][:, 0], ALU.subtract).then_inc(o_lo, 1)

            low(0, 0)
            pool.wait_ge(b_loaded, 16)
            with_bias(0, 0)

            def body(i, s):
                if before(i, NCH - 1):
                    low(i + 1, 1 - s)
                    with_bias(i + 1, 1 - s)
            tiles(pool, NCH, 2, body)

        @block.vector
        def _(dve):
            dve.wait_ge(w_hi, 1)
            nc.vector.tensor_tensor(W[:, 1], stage[:], W[:, 0], ALU.subtract).then_inc(w_lo, 1)

            def body(i, s):
                link = steps(dve, dv, i * NORM_LINKS)
                for nt in range(4):
                    n = i * 4 + nt
                    row = x2[s][:, nt, :]
                    if nt == 0 and at_least(i, 2):
                        dve.wait_ge(x_stored[s], (i - s) * 8)
                    if nt == 0:
                        dve.wait_ge(g_loaded[s], (i - s) * 8 + 16)
                    dve.wait_ge(p_done, n + 1)
                    nc.vector.tensor_tensor(row, pp[nt][:], gate[s][:], ALU.mult).then_inc(p_read, 1)
                    if nt == 0:
                        dve.wait_ge(xb_ready, i + 1)
                    dve.wait_ge(p_read, n + 1)
                    nc.vector.tensor_tensor(row, row, xr[s][:, nt, :], ALU.add).then_inc(x2_ready, 1)
                dve.wait_ge(x2_ready, i * 4 + 4)
                norm_rows(nc, dve, link, x2[s], stats, mv, rstd, tmp, var_ready, root_ready, i)
                if at_least(i, 1):
                    dve.wait_ge(tr_done, i * 4)
                for nt in range(4):
                    last = nc.vector.tensor_scalar(xn[:, nt, :], x2[s][:, nt, :], mv[:, nt, 0:1], rstd[:, nt:nt + 1],
                                                   ALU.subtract, ALU.mult)
                last.then_inc(xn_ready, 1)
            tiles(dve, NCH, 2, body)

        @block.tensor
        def _(pe):
            def project(i, s):
                pe.wait_ge(o_lo, i + 1)
                for nt in range(4):
                    if at_least(i, 1):
                        pe.wait_ge(p_read, i * 4 + nt - 3)
                    for n, (k, w) in enumerate(PASSES):
                        for c in range(DC):
                            last = nc.tensor.matmul(pp[nt][:], os_[s][:, k, c, nt * P:(nt + 1) * P], W[:, w, c, :],
                                                    start=n + c == 0, stop=n == 2 and c == DC - 1)
                    last.then_inc(p_done, 1)

            pe.wait_ge(w_lo, 1)
            project(0, 0)

            def body(i, s):
                if before(i, NCH - 1):
                    project(i + 1, 1 - s)
                pe.wait_ge(xn_ready, i + 1)
                for c in range(DC):
                    if at_least(i, 1):
                        pe.wait_ge(h_ready, i * 4 + c - 3)
                    for nt in range(4):
                        last = nc.tensor.transpose(pT[c][:, nt * P:(nt + 1) * P], xn[:, nt, c * P:(c + 1) * P], ident[:])
                    last.then_inc(tr_done, 1)
            tiles(pe, NCH, 2, body)


def mlp_phase(nc, io, keep):
    with ExitStack() as ctx:
        m = Mem(nc, ctx, "mlp")
        NCH = B * S // 512
        cols = keep["cols"]
        W1 = m.sb("W1", [P, 2, DC, MLP], F32R)
        W2 = m.sb("W2", [P, 2, MC, D], F32R)
        b2 = m.sb("b2", [P, D])
        gate = [m.sb(f"gate{i}", [P, D]) for i in range(2)]
        hs = [m.sb(f"hs{i}", [P, 2, DC, 512], F32R) for i in range(2)]
        hf = [m.sb(f"hf{i}", [P, 512]) for i in range(2)]
        xr = [m.sb(f"xr{i}", [P, 4, D]) for i in range(2)]
        tu = [m.sb(f"tu{i}", [P, 512]) for i in range(2)]
        us = [m.sb(f"us{i}", [P, 2, 512], F32R) for i in range(2)]
        y = [m.sb(f"y{i}", [P, D]) for i in range(4)]
        pu = [m.ps(f"pu{i}") for i in range(4)]
        pa = [m.ps(f"pa{i}") for i in range(4)]

        w_loaded, b_loaded, w_hi, w_lo = m.sems("w_loaded", 2), m.sem("b_loaded"), m.sem("w_hi"), m.sem("w_lo")
        h_loaded, x_loaded, g_loaded, stored = m.sems("h_loaded", 2), m.sems("x_loaded", 2), m.sems("g_loaded", 2), m.sems("stored", 4)
        h_hi, h_lo = m.sem("h_hi"), m.sem("h_lo")
        u_done, u_hi, u_lo, u_used, a_done, a_read, gated, y_ready = [
            m.sem(x) for x in ("u_done", "u_hi", "u_lo", "u_used", "a_done", "a_read", "gated", "y_ready")]
        block = m.block()
        NP = 8
        def piece(n):
            if n % 2 == 0:
                return lambda k: W1[:, k, :, n // 2 * 512:(n // 2 + 1) * 512]
            return lambda k: W2[:, k, n // 2 * 4:(n // 2 + 1) * 4, :]

        H_STEPS = (10, 11, 12, 13)

        def pieces_behind(i, j):
            first = j // 2 + 2
            return (first, first + 1) if isinstance(i, int) and i == 0 and j % 4 == 1 and first < NP else ()

        @block.sync
        def _(sp):
            def load_h(i, c):
                if c >= 2 or at_least(i, 1):
                    sp.wait_ge(h_lo, i * 4 + c - 1)
                sp.dma_start(hf[c % 2][:], io["h2_d"][c * P:(c + 1) * P, bass.ds(i * 512, 512)]).then_inc(h_loaded[c % 2], 16)

            def load_x(i, s):
                at = bass.ds(i * 512, 512)
                sp.dma_start(xr[s][:], io["x2_d"][at, :].rearrange("(n p) d -> p n d", p=P)).then_inc(x_loaded[s], 16)
                sp.dma_start(gate[s][:], io["gate_d"][1, bass.ds(i, 1)].rearrange("a p d -> (a p) d")).then_inc(g_loaded[s], 16)

            load_h(0, 0)
            load_h(0, 1)
            for n in range(NP):
                if n >= 2:
                    sp.wait_ge(w_lo, n - 1)
                at = slice(n // 2 * 512, (n // 2 + 1) * 512)
                src = io["W1"][:, at] if n % 2 == 0 else io["W2"][at, :]
                src = src.rearrange("(a p) d -> p a d", p=P)
                sp.dma_start(xr[n % 2][:], src).then_inc(w_loaded[n % 2], 16)
                if n == 0:
                    load_h(0, 2)
                    load_h(0, 3)
                if n == 1:
                    sp.dma_start(b2[:], io["rows"][7:8, :].to_broadcast([P, D])).then_inc(b_loaded, 16)
            load_h(1, 0)
            load_h(1, 1)
            sp.wait_ge(w_lo, NP)
            load_x(0, 0)
            load_x(1, 1)

            def body(i, s):
                if before(i, NCH - 1):
                    load_h(i + 1, 2)
                    load_h(i + 1, 3)
                if before(i, NCH - 2):
                    load_h(i + 2, 0)
                    load_h(i + 2, 1)
                for nt in range(4):
                    sp.wait_ge(y_ready, i * 4 + nt + 1)
                    sp.dma_start(io["out"][bass.ds(i * 512 + nt * P, P), :], y[nt][:]).then_inc(stored[nt], 16)
                if before(i, NCH - 2):
                    load_x(i + 2, s)
            tiles(sp, NCH, 2, body)
            for x in stored:
                sp.wait_ge(x, 16 * NCH)

        @block.scalar
        def _(act):
            def split_high(n):
                act.wait_ge(w_loaded[n % 2], 16 * (n // 2 + 1))
                nc.scalar.activation(piece(n)(0), xr[n % 2][:], ACT.Identity).then_inc(w_hi, 1)

            def h_high(i, s, c):
                act.wait_ge(h_loaded[c % 2], (i * 2 + c // 2 + 1) * 16)
                nc.scalar.activation(hs[s][:, 0, c, :], hf[c % 2][:], ACT.Identity).then_inc(h_hi, 1)

            for c in range(DC):
                h_high(0, 0, c)
            split_high(0)
            split_high(1)

            def body(i, s):
                for j in range(MC):
                    n = i * MC + j
                    act.wait_ge(u_done, n + 1)
                    if j >= 2 or at_least(i, 1):
                        act.wait_ge(u_lo, n - 1)
                    if j >= 2:
                        act.wait_ge(u_used, i * (MC - 1) + j - 1)
                    elif j == 1 and at_least(i, 1):
                        act.wait_ge(a_done, i * 4)
                    elif at_least(i, 1):
                        act.wait_ge(u_used, i * (MC - 1))
                    bias = cols[:, COLS["b1"][0] + j:COLS["b1"][0] + j + 1]
                    nc.scalar.activation(tu[j % 2][:], pu[j % 4][:], ACT.Gelu, bias=bias)
                    nc.scalar.activation(us[j % 2][:, 0, :], pu[j % 4][:], ACT.Gelu, bias=bias).then_inc(u_hi, 1)
                    for w in pieces_behind(i, j):
                        split_high(w)
                    if j in H_STEPS and before(i, NCH - 1):
                        h_high(i + 1, 1 - s, H_STEPS.index(j))
            tiles(act, NCH, 2, body)

        @block.gpsimd
        def _(pool):
            def body(i, s):
                for c in range(DC):
                    pool.wait_ge(h_hi, i * 4 + c + 1)
                    nc.gpsimd.tensor_tensor(hs[s][:, 1, c, :], hf[c % 2][:], hs[s][:, 0, c, :], ALU.subtract).then_inc(h_lo, 1)
            tiles(pool, NCH, 2, body)

        @block.vector
        def _(dve):
            def split_low(n):
                dve.wait_ge(w_hi, n + 1)
                nc.vector.tensor_tensor(piece(n)(1), xr[n % 2][:], piece(n)(0), ALU.subtract).then_inc(w_lo, 1)

            split_low(0)
            split_low(1)
            dve.wait_ge(b_loaded, 16)

            def low(n, j):
                dve.wait_ge(u_hi, n + 1)
                nc.vector.tensor_tensor(us[j % 2][:, 1, :], tu[j % 2][:], us[j % 2][:, 0, :], ALU.subtract).then_inc(u_lo, 1)

            def outputs(i, s):
                dve.wait_ge(x_loaded[s], (i - s) * 8 + 16)
                dve.wait_ge(g_loaded[s], (i - s) * 8 + 16)
                for nt in range(4):
                    dve.wait_ge(a_done, i * 4 + nt + 1)
                    if at_least(i, 1):
                        dve.wait_ge(stored[nt], i * 16)
                    nc.vector.tensor_tensor(y[nt][:], pa[nt][:], b2[:], ALU.add).then_inc(a_read, 1)
                for nt in range(4):
                    dve.wait_ge(a_read, i * 4 + nt + 1)
                    nc.vector.tensor_tensor(y[nt][:], y[nt][:], gate[s][:], ALU.mult).then_inc(gated, 1)
                for nt in range(4):
                    dve.wait_ge(gated, i * 4 + nt + 1)
                    nc.vector.tensor_tensor(y[nt][:], y[nt][:], xr[s][:, nt, :], ALU.add).then_inc(y_ready, 1)

            low(0, 0)

            def body(i, s):
                for j in range(1, MC):
                    low(i * MC + j, j)
                    for w in pieces_behind(i, j):
                        split_low(w)
                if before(i, NCH - 1):
                    low((i + 1) * MC, 0)
                outputs(i, s)
            tiles(dve, NCH, 2, body)

        @block.tensor
        def _(pe):
            def hidden(i, s, j):
                n = i * MC + j
                if j == 0:
                    pe.wait_ge(h_lo, i * 4 + 4)
                if isinstance(i, int) and i == 0 and j % 4 == 0:
                    pe.wait_ge(w_lo, j // 2 + 1)
                if j >= 4 or at_least(i, 1):
                    pe.wait_ge(u_hi, n - 3)
                for q, (k, w) in enumerate(PASSES):
                    for c in range(DC):
                        last = nc.tensor.matmul(pu[j % 4][:], W1[:, k, c, j * P:(j + 1) * P], hs[s][:, w, c, :],
                                                start=q + c == 0, stop=q == 2 and c == DC - 1)
                last.then_inc(u_done, 1)

            hidden(0, 0, 0)

            def body(i, s):
                for j in range(MC):
                    if j < MC - 1:
                        hidden(i, s, j + 1)
                    elif before(i, NCH - 1):
                        hidden(i + 1, 1 - s, 0)
                    if isinstance(i, int) and i == 0 and j % 4 == 0:
                        pe.wait_ge(w_lo, j // 2 + 2)
                    pe.wait_ge(u_lo, i * MC + j + 1)
                    for nt in range(4):
                        if j == 0 and at_least(i, 1):
                            pe.wait_ge(a_read, i * 4 + nt - 3)
                        for q, (k, w) in enumerate(PASSES):
                            last = nc.tensor.matmul(pa[nt][:], us[j % 2][:, k, nt * P:(nt + 1) * P], W2[:, w, j, :],
                                                    start=j + q == 0, stop=j == MC - 1 and q == 2)
                        if j == MC - 1:
                            last.then_inc(a_done, 1)
                    if j < MC - 1:
                        last.then_inc(u_used, 1)
            tiles(pe, NCH, 2, body)


def build(nc, io, upto=9):
    for name, shape, dt in [("x1_d", (B * S, D), F32), ("gate_d", (2, B * S // 512, P, D), F32),
                            ("qk_d", (2, 2, D, B * S), F32), ("v_d", (B * S, D), F32),
                            ("o_d", (D, B * S), F32), ("x2_d", (B * S, D), F32), ("h2_d", (D, B * S), F32)]:
        io[name] = nc.dram_tensor(name, shape, dt, kind="Internal").ap()
    with ExitStack() as ctx:
        m = Mem(nc, ctx, "keep")
        keep = {"cols": m.sb("cols", [P, NCOLS]), "ident": m.sb("ident", [P, P]),
                "modA": m.sb("modA", [P, 2, B * S // 512 * DC]), "modB": m.sb("modB", [P, 2, B * S // 512 * DC])}
        with ExitStack() as early:
            e = Mem(nc, early, "graph")
            keep["floor4"] = e.sb("floor4", [4, 1])
            keep["wl_bc"] = e.sb("wl_bc", [P, 2 * NONGT * L])
            keep["bb"] = e.sb("bb", [P, 1])
            keep["LW"] = e.sb("LW", [P, 2, B, DC, D + 2 * HM], F32R)
            keep["VB"] = e.sb("VB", [GM, B, 2, DC, P])
            keep["r4"] = e.sb("r4", [4, B, D + 2 * HM], F32R)
            setup_phase(nc, io, keep)
            graph_phase(nc, io, keep)
        if upto > 1:
            qkv_phase(nc, io, keep)
        if upto > 2:
            attention_phase(nc, io, keep)
        if upto > 3:
            proj_phase(nc, io, keep)
        if upto > 4:
            mlp_phase(nc, io, keep)


_OUT = [((B, S, D), "float32")]


def layouts(inp):
    a = {k: np.asarray(v) for k, v in inp.items()}
    x, mask = a["x"], a["mask_BxSxSx11_ik0"]

    def columns(v):
        return np.ascontiguousarray(v.reshape(-1, P).T)
    bqkv, bt = a["L1_cond_bqkv"], a["L1_cond_bt"]
    cols = np.concatenate([
        a["cond_1024"].reshape(B, DC, P).transpose(2, 1, 0).reshape(P, DC * B), columns(a["L0_cond_b_self"]),
        columns(a["L0_cond_bq"]), columns(a["L0_cond_bk"]), columns(bqkv[:2 * D]),
        columns(a["L1_cond_g1"]), columns(a["L1_cond_g2"]), columns(a["L1_cond_be1"]), columns(a["L1_cond_be2"]),
        columns(a["L1_cond_b1"]), columns(bt)], axis=1)
    rows = np.stack([a["L0_cond_b_self"], a["L0_cond_bout"][0], a["L0_cond_bout"][1], bt[2 * D:3 * D], bt[5 * D:6 * D],
                     bqkv[2 * D:], a["L1_cond_bproj"], a["L1_cond_b2"]])
    near = np.stack([mask[:, :, :NONGT, :], mask[:, :NONGT, :, :].swapaxes(1, 2)], axis=2)
    wl = np.concatenate([np.tile(a["L0_cond_w_bias"], 2 * NONGT), a["L0_cond_b_bias"].reshape(1)])[None]
    out = {
        "x": x.reshape(B * S, D), "xT": x.transpose(0, 2, 1), "mask": near.reshape(B * S, 2 * NONGT * L),
        "cols": cols, "rows": rows, "wl": wl,
        "ident": np.eye(P, dtype=np.float32), "floor4": np.array([[0], [0], [1], [1]], np.float32),
        "Wself": a["L0_cond_W_self"], "WselfT": a["L0_cond_W_self"].T,
        "Wq": a["L0_cond_Wq"], "WkT": a["L0_cond_Wk"].transpose(0, 2, 1),
        "WoutT": a["L0_cond_Wout"].reshape(2, D, D).transpose(0, 2, 1),
        "Wqkv": a["L1_cond_Wqkv"], "Wproj": a["L1_cond_Wproj"], "W1": a["L1_cond_W1"], "W2": a["L1_cond_W2"], "Wt": a["L1_cond_Wt"],
    }
    return {k: np.ascontiguousarray(v) for k, v in out.items()}


def kernel(**inputs):
    import concourse.bacc as bacc
    from concourse.bass_utils import run_bass_kernel_spmd

    nc = bacc.Bacc("TRN2", target_bir_lowering=False, num_devices=1)
    arrays = layouts(inputs)
    io = {k: nc.dram_tensor(f"in_{k}", v.shape, mybir.dt.from_np(v.dtype), kind="ExternalInput").ap() for k, v in arrays.items()}
    io["out"] = nc.dram_tensor("out", (B * S, D), F32, kind="ExternalOutput").ap()
    build(nc, io)
    r = run_bass_kernel_spmd(nc, [{f"in_{k}": v for k, v in arrays.items()}], core_ids=[0])
    return r.results[0]["out"].reshape(B, S, D)
```
